# Optimizing a Trainium2 kernel written in Bass

```python
import numpy as np
import jax
import jax.numpy as jnp

def _softmax(x, axis=-1):
    return jax.nn.softmax(x, axis=axis)

def _gelu(x):
    return jax.nn.gelu(x, approximate=True)

def _silu(x):
    return jax.nn.silu(x)

def _sigmoid(x):
    return jax.nn.sigmoid(x)

def _layernorm(x, axis=-1, eps=1e-05):
    m = jnp.mean(x, axis=axis, keepdims=True)
    v = jnp.var(x, axis=axis, keepdims=True)
    return (x - m) / jnp.sqrt(v + eps)

def _scatter_add(tgt, idx, src, axis=0):
    return tgt.at[idx].add(src)

def _segment_sum(src, seg, n):
    return jax.ops.segment_sum(src, seg, n)
kernel_name = 'mk_adaln_d1_jaxref_r8_3dc76e'

def setup_inputs(seed: int=0):
    np.random.seed(seed)
    _w = jnp.asarray

    def _L0_attn_setup():
        import jax, jax.numpy as jnp
        import numpy as np
        B, L, H = (8, 256, 128)
        MASK_IDENTITY = True
        key = jax.random.key(seed)
        ks = jax.random.split(key, 7)
        s = 1.0 / np.sqrt(H)
        return {'x': jax.random.normal(ks[0], (B, L, H), dtype=jnp.float32), 'Wq': jax.random.uniform(ks[1], (H, H), jnp.float32, -s, s), 'bq': jax.random.uniform(ks[2], (H,), jnp.float32, -s, s), 'Wk': jax.random.uniform(ks[3], (H, H), jnp.float32, -s, s), 'bk': jax.random.uniform(ks[4], (H,), jnp.float32, -s, s), 'Wv': jax.random.uniform(ks[5], (H, H), jnp.float32, -s, s), 'bv': jax.random.uniform(ks[6], (H,), jnp.float32, -s, s)}
    _L0_attn_in = _L0_attn_setup()

    def _L0_ffn_setup():
        import jax, jax.numpy as jnp
        import numpy as np
        H = 128
        I = 256
        E = 8
        B, S = (2, 512)
        EPS = 1e-05
        INIT = 0.02

        def _layernorm(x, w, b):
            mu = jnp.mean(x, axis=-1, keepdims=True)
            var = jnp.mean(jnp.square(x - mu), axis=-1, keepdims=True)
            return (x - mu) * jax.lax.rsqrt(var + EPS) * w + b
        key = jax.random.key(seed)
        ks = jax.random.split(key, 9)
        return {'hidden_states': jax.random.normal(ks[0], (B, S, H), jnp.float32), 'ln_w': jnp.ones((H,), jnp.float32), 'ln_b': jnp.zeros((H,), jnp.float32), 'router_w': jax.random.normal(ks[1], (H, E), jnp.float32) * INIT, 'gate_w': jax.random.normal(ks[2], (E, H, I), jnp.float32) * INIT, 'up_w': jax.random.normal(ks[3], (E, H, I), jnp.float32) * INIT, 'down_w': jax.random.normal(ks[4], (E, I, H), jnp.float32) * INIT, 'sh_gate': jax.random.normal(ks[5], (H, I), jnp.float32) * INIT, 'sh_up': jax.random.normal(ks[6], (H, I), jnp.float32) * INIT, 'sh_down': jax.random.normal(ks[7], (I, H), jnp.float32) * INIT}
    _L0_ffn_in = _L0_ffn_setup()
    _L0_c = _w((lambda *s: np.random.randn(*s).astype(np.float32) * 0.05)(4, 128))
    _L0_wmod = _w((lambda *s: np.random.randn(*s).astype(np.float32) * 0.05)(128, 6 * 128) * 128 ** (-0.5))
    _d = {'L0_attn_x': _L0_attn_in['x'], 'L0_attn_Wq': _L0_attn_in['Wq'], 'L0_attn_bq': _L0_attn_in['bq'], 'L0_attn_Wk': _L0_attn_in['Wk'], 'L0_attn_bk': _L0_attn_in['bk'], 'L0_attn_Wv': _L0_attn_in['Wv'], 'L0_attn_bv': _L0_attn_in['bv'], 'L0_ffn_ln_w': _L0_ffn_in['ln_w'], 'L0_ffn_ln_b': _L0_ffn_in['ln_b'], 'L0_ffn_router_w': _L0_ffn_in['router_w'], 'L0_ffn_gate_w': _L0_ffn_in['gate_w'], 'L0_ffn_up_w': _L0_ffn_in['up_w'], 'L0_ffn_down_w': _L0_ffn_in['down_w'], 'L0_ffn_sh_gate': _L0_ffn_in['sh_gate'], 'L0_ffn_sh_up': _L0_ffn_in['sh_up'], 'L0_ffn_sh_down': _L0_ffn_in['sh_down'], 'L0_c': _L0_c, 'L0_wmod': _L0_wmod}
    _x0 = _d['L0_attn_x']
    _d['L0_attn_x'] = jax.random.normal(jax.random.fold_in(jax.random.key(seed), 1), (4, 512, 128), dtype=_x0.dtype)
    del _x0
    return _d

def reference(L0_attn_x, L0_attn_Wq, L0_attn_bq, L0_attn_Wk, L0_attn_bk, L0_attn_Wv, L0_attn_bv, L0_ffn_ln_w, L0_ffn_ln_b, L0_ffn_router_w, L0_ffn_gate_w, L0_ffn_up_w, L0_ffn_down_w, L0_ffn_sh_gate, L0_ffn_sh_up, L0_ffn_sh_down, L0_c, L0_wmod):

    def _L0_attn_ref(x, Wq, bq, Wk, bk, Wv, bv):
        import jax, jax.numpy as jnp
        import numpy as np
        B, L, H = (8, 256, 128)
        MASK_IDENTITY = True
        q = jnp.einsum('blh,oh->blo', x, Wq) + bq
        k = jnp.einsum('blh,oh->blo', x, Wk) + bk
        v = jnp.einsum('blh,oh->blo', x, Wv) + bv
        hidden = q.shape[-1]
        attn = jnp.einsum('blh,bmh->blm', q / hidden, k)
        if MASK_IDENTITY:
            mask_value = -jnp.finfo(attn.dtype).max
            eye = jnp.eye(attn.shape[-1], dtype=bool)
            attn = jnp.where(eye[None, :, :], mask_value, attn)
        attn = jax.nn.softmax(attn, axis=-1)
        return jnp.einsum('blm,bmh->blh', attn, v)

    def _L0_ffn_ref(hidden_states, ln_w, ln_b, router_w, gate_w, up_w, down_w, sh_gate, sh_up, sh_down):
        import jax, jax.numpy as jnp
        import numpy as np
        H = 128
        I = 256
        E = 8
        B, S = (2, 512)
        EPS = 1e-05
        INIT = 0.02

        def _layernorm(x, w, b):
            mu = jnp.mean(x, axis=-1, keepdims=True)
            var = jnp.mean(jnp.square(x - mu), axis=-1, keepdims=True)
            return (x - mu) * jax.lax.rsqrt(var + EPS) * w + b
        b, s, h = hidden_states.shape
        normed = _layernorm(hidden_states, ln_w, ln_b)
        xf = normed.reshape(-1, h)
        logits = xf @ router_w
        top_idx = jnp.argmax(logits, axis=-1)
        top_score = jax.nn.sigmoid(jnp.max(logits, axis=-1))

        def body(acc, ew):
            g, u, d, e = ew
            w = jnp.where(top_idx == e, top_score, 0.0)[:, None]
            xe = xf * w
            hmid = jax.nn.silu(xe @ g) * (xe @ u)
            return (acc + hmid @ d, None)
        routed, _ = jax.lax.scan(body, jnp.zeros_like(xf), (gate_w, up_w, down_w, jnp.arange(E)))
        shared = jax.nn.silu(xf @ sh_gate) * (xf @ sh_up) @ sh_down
        moe_out = (routed + shared).reshape(b, s, h)
        return hidden_states + moe_out
    x = L0_attn_x
    mod = (_silu(L0_c) @ L0_wmod).reshape(L0_c.shape[0], 6, 1, -1)
    sa, ca, ga, sb, cb, gb = (mod[:, 0], mod[:, 1], mod[:, 2], mod[:, 3], mod[:, 4], mod[:, 5])
    ga = (2 * (ga >= 0) - 1) * jnp.maximum(jnp.abs(ga), 0.25)
    gb = (2 * (gb >= 0) - 1) * jnp.maximum(jnp.abs(gb), 0.25)
    h = _layernorm(x, axis=-1) * (1 + ca) + sa
    x = x + ga * _L0_attn_ref(h, L0_attn_Wq, L0_attn_bq, L0_attn_Wk, L0_attn_bk, L0_attn_Wv, L0_attn_bv)
    h = _layernorm(x, axis=-1) * (1 + cb) + sb
    x = x + gb * _L0_ffn_ref(h, L0_ffn_ln_w, L0_ffn_ln_b, L0_ffn_router_w, L0_ffn_gate_w, L0_ffn_up_w, L0_ffn_down_w, L0_ffn_sh_gate, L0_ffn_sh_up, L0_ffn_sh_down)
    return x

_drawn_inputs = setup_inputs


def setup_inputs(seed=0):
    import zlib

    import numpy as np

    out = dict(_drawn_inputs(seed))
    spreads = {'L0_ffn_ln_w': (1.0, 0.6), 'L0_ffn_ln_b': (0.0, 0.8)}
    factors = {'L0_attn_Wq': 8.0,
     'L0_attn_bq': 8.0,
     'L0_attn_Wk': 8.0,
     'L0_attn_bk': 8.0,
     'L0_attn_Wv': 8.0,
     'L0_attn_bv': 4.284,
     'L0_ffn_router_w': 8.0,
     'L0_ffn_gate_w': 8.0,
     'L0_ffn_up_w': 8.0,
     'L0_ffn_down_w': 8.0,
     'L0_ffn_sh_gate': 8.0,
     'L0_ffn_sh_up': 8.0,
     'L0_ffn_sh_down': 8.0}
    for name, (base, spread) in spreads.items():
        noise = np.random.default_rng([zlib.crc32(name.encode()), seed]).standard_normal(out[name].shape)
        drawn = base * np.exp(spread * noise) if base else spread * noise
        out[name] = jnp.asarray(drawn.astype(out[name].dtype))
    for name, factor in factors.items():
        out[name] = (out[name] * factor).astype(out[name].dtype)
    return out
```

```python
from contextlib import ExitStack

import concourse.bass as bass
from concourse import mybir

F32 = mybir.dt.float32
BF16 = mybir.dt.bfloat16
I32 = mybir.dt.int32
ALU = mybir.AluOpType
ACT = mybir.ActivationFunctionType
AX_X = mybir.AxisListType.X

P = 128
B = 4
L = 512
H = 128
T = L // P
NT = B * T
E = 8
I = 256
IC = I // P
NS = NT + E - 1
ZW = H + 1
EPS = 1e-5
LOWEST = -3.3895313892515355e38
RSQRT_MAGIC = float(0x5F3759DF)
SKIP = 4096.0


class Steps:

    def __init__(self, eng, sem):
        self.eng, self.sem, self.count = eng, sem, 0

    def then(self, instruction):
        instruction.then_inc(self.sem, 1)
        self.count += 1

    def done(self):
        self.eng.wait_ge(self.sem, self.count)

    def chain(self, instruction):
        self.then(instruction)
        self.done()


def adaln_block(nc, x, vecs, bv, wmod, wqkv, router_w, w_gu, w_down, sh_gu, sh_down, out):
    z_rows = nc.dram_tensor("z_rows", [B * L, ZW], F32).ap()
    y_rows = nc.dram_tensor("y_rows", [B * L, H], F32).ap()

    ctx = ExitStack()
    with ctx:
        def sb(name, shape, dt=F32):
            return ctx.enter_context(nc.sbuf_tensor(name, shape, dt))

        def bank(name):
            return ctx.enter_context(nc.psum_tensor(name, [P, 512], F32))

        def sem(name):
            return ctx.enter_context(nc.semaphore(name))

        x_in = sb("x_in", [P, NT, H])
        vec_rows = sb("vec_rows", [8, H])
        bv_rows = sb("bv_rows", [B, H])
        wmod_sb = sb("wmod_sb", [P, 6 * H])
        wqkv_sb = sb("wqkv_sb", [P, 3, H])
        router_sb = sb("router_sb", [P, E])
        w_gu_sb = sb("w_gu_sb", [P, E * 2 * I])
        w_down_sb = sb("w_down_sb", [P, E * IC * H])
        sh_gu_sb = sb("sh_gu_sb", [P, 2 * I])
        sh_down_sb = sb("sh_down_sb", [P, IC, H])
        ident = sb("ident", [P, P])
        ident_b = sb("ident_b", [P, P], BF16)
        mask_diag = sb("mask_diag", [P, P], BF16)
        before = sb("before", [P, P], BF16)
        ones_b = sb("ones_b", [P, P], BF16)
        iota_p = sb("iota_p", [P, P])
        iota_e = sb("iota_e", [P, E])
        iota_e8 = sb("iota_e8", [P, E])
        iota_s = sb("iota_s", [P, NS])
        steps_128 = sb("steps_128", [P, NT])
        earlier_e = sb("earlier_e", [P, E, E])
        batch_512 = sb("batch_512", [P, NT])
        tile_8 = sb("tile_8", [P, NT])
        part_4 = sb("part_4", [P, 1])
        pick_b = sb("pick_b", [B, B, P])
        cols = sb("cols", [P, 8])
        bq_h = sb("bq_h", [P, 1])
        silu_c = sb("silu_c", [P, B])
        shift_a = sb("shift_a", [P, B])
        scale_a = sb("scale_a", [P, B])
        mod_raw = sb("mod_raw", [B, 4, H])
        gate_sign = sb("gate_sign", [B, 2, H])
        gate_abs = sb("gate_abs", [B, 2, H])
        gate_half = sb("gate_half", [B, 2, H])
        mod_rows = sb("mod_rows", [B, 5, H])
        bc = sb("bc", [P, B, 4, H])
        wv_ga = sb("wv_ga", [P, B, H])
        sh_down_gb = sb("sh_down_gb", [P, B, IC, H])
        st1 = sb("st1", [P, NT, 6])
        mv1 = sb("mv1", [P, NT, 2])
        v1 = sb("v1", [P, NT])
        t1 = sb("t1", [P, NT])
        r1 = sb("r1", [P, NT])
        normed = sb("normed", [P, T, H])
        hT = sb("hT", [P, L])
        qT = sb("qT", [P, L])
        kT = sb("kT", [P, L])
        v_sb = sb("v_sb", [P, 2, T, H])
        neg_max = sb("neg_max", [P, NT])
        probs = sb("probs", [P, 2, L])
        prob_sum = sb("prob_sum", [P, NT])
        prob_inv = sb("prob_inv", [P, NT])
        probsT = sb("probsT", [P, 2, L])
        x_res = sb("x_res", [P, NT, H])
        x1 = sb("x1", [P, NT, H])
        st2 = sb("st2", [P, NT, 6])
        mv2 = sb("mv2", [P, NT, 2])
        v2 = sb("v2", [P, NT])
        t2 = sb("t2", [P, NT])
        r2 = sb("r2", [P, NT])
        h2u = sb("h2u", [P, NT, H])
        h2 = sb("h2", [P, NT, H])
        st3 = sb("st3", [P, NT, 6])
        mv3 = sb("mv3", [P, NT, 2])
        v3 = sb("v3", [P, NT])
        t3 = sb("t3", [P, NT])
        r3 = sb("r3", [P, NT])
        zw = sb("zw", [P, NT, ZW])
        gh2 = sb("gh2", [P, T, H])
        xb = sb("xb", [P, NT, H])
        base = sb("base", [P, NT, H])
        xfT = sb("xfT", [P, B, L])
        top = sb("top", [P, NT])
        exp_top = sb("exp_top", [P, NT])
        exp_top1 = sb("exp_top1", [P, NT])
        is_top = sb("is_top", [P, NT, E])
        cand = sb("cand", [P, NT, E])
        first = sb("first", [P, NT])
        onehot = sb("onehot", [P, NT, E])
        onehot_b = sb("onehot_b", [P, NT, E], BF16)
        seen = sb("seen", [P, B + 1, E], BF16)
        seen_new = sb("seen_new", [P, B, E])
        rank_of = sb("rank_of", [P, NT, E])
        rank = sb("rank", [P, NT])
        rank_i = sb("rank_i", [P, NT], I32)
        rank_div_i = sb("rank_div_i", [P, NT], I32)
        rank_div = sb("rank_div", [P, NT])
        rank_mod = sb("rank_mod", [P, NT])
        row_hot = sb("row_hot", [P, NT, P], BF16)
        count = sb("count", [P, E])
        count_over = sb("count_over", [P, E, NT])
        slots_of = sb("slots_of", [P, E])
        slots_before = sb("slots_before", [P, E, E])
        slot0 = sb("slot0", [P, E])
        slot_end = sb("slot_end", [P, E])
        slot_pick = sb("slot_pick", [P, NT, E])
        slot_first = sb("slot_first", [P, NT])
        slot = sb("slot", [P, NT])
        slot_diff = sb("slot_diff", [P, NT, NS])
        slot_val = sb("slot_val", [P, NT, 3, NS], BF16)
        table = sb("table", [P, 3, NS])
        token_ab = sb("token_ab", [P, NS])
        token = sb("token", [P, NS])
        no_token = sb("no_token", [P, NS])
        gather_i = sb("gather_i", [P, NS], I32)
        scatter_i = sb("scatter_i", [P, NS], I32)
        slot_past = sb("slot_past", [P, NS, E])
        slot_exp = sb("slot_exp", [P, NS])
        slot_exp_i = sb("slot_exp_i", [P, NS], I32)
        sh_silu = sb("sh_silu", [P, IC, L])
        sh_hid = sb("sh_hid", [P, IC, L])
        zg = sb("zg", [P, NS, ZW])
        xsT = sb("xsT", [P, 2, P])
        sl_silu = sb("sl_silu", [P, 2, I])
        sl_hid = sb("sl_hid", [P, 2, I])
        sl_hidT = sb("sl_hidT", [P, 2, IC, P])
        y_sl = sb("y_sl", [P, NS, H])
        y_tok, gy, o_sb = x_in, x_res, h2u

        S = [bank("S0"), bank("S1")]
        PT = [bank("PT0"), bank("PT1")]
        O = [bank("O0"), bank("O1")]
        M = [bank("M0"), bank("M1")]

        ld_x = [sem(f"ld_x{b}") for b in range(B)]
        ld_vec, ld_bv, ld_wmod, ld_wqkv = sem("ld_vec"), sem("ld_bv"), sem("ld_wmod"), sem("ld_wqkv")
        ld_router, ld_sh_gu, ld_sh_down = sem("ld_router"), sem("ld_sh_gu"), sem("ld_sh_down")
        ld_gu, ld_down = sem("ld_gu"), sem("ld_down")
        c_set = sem("c_set")
        c_done = sem("c_done")
        vec_up, cols_done, silu_done = sem("vec_up"), sem("cols_done"), sem("silu_done")
        modc_up, modc_done = sem("modc_up"), sem("modc_done")
        modr_up, modr_raw, modr_done = sem("modr_up"), sem("modr_raw"), sem("modr_done")
        row_up, bc_done, ga_up, wv_done = sem("row_up"), sem("bc_done"), sem("ga_up"), sem("wv_done")
        shd_done = sem("shd_done")
        st1_done, mv1_done, norm_done = sem("st1_done"), sem("mv1_done"), sem("norm_done")
        r1_done = sem("r1_done")
        nT_up, hT_done = sem("nT_up"), sem("hT_done")
        q_up, qT_done, k_up, kT_done, v_up, v_done = (sem(n) for n in ("q_up", "qT_done", "k_up", "kT_done", "v_up", "v_done"))
        s_up, max_done, p_done = sem("s_up"), sem("max_done"), sem("p_done")
        pT_up, pT_done, o_up, x1_done = sem("pT_up"), sem("pT_done"), sem("o_up"), sem("x1_done")
        xres_done = sem("xres_done")
        inv_done = sem("inv_done")
        st2_done, mv2_done, h2u_done, h2_done = sem("st2_done"), sem("mv2_done"), sem("h2u_done"), sem("h2_done")
        st3_done, mv3_done, z_done, w_done = sem("st3_done"), sem("mv3_done"), sem("z_done"), sem("w_done")
        gh2_done, xb_done = sem("gh2_done"), sem("xb_done")
        zT_up, xfT_done, lg_up, top_done, exp_done = sem("zT_up"), sem("xfT_done"), sem("lg_up"), sem("top_done"), sem("exp_done")
        lg_read = sem("lg_read")
        hot_done, hotb_done, seen_sum, seen_done = sem("hot_done"), sem("hotb_done"), sem("seen_sum"), sem("seen_done")
        rank_up, rank_read, rmod_done, rowhot_done = sem("rank_up"), sem("rank_read"), sem("rmod_done"), sem("rowhot_done")
        z_stored = sem("z_stored")
        cnt_up, cnt_read, sval_done, table_up, table_read = sem("cnt_up"), sem("cnt_read"), sem("sval_done"), sem("table_up"), sem("table_read")
        gidx_done, sidx_done, sexp_done = sem("gidx_done"), sem("sidx_done"), sem("sexp_done")
        shg_up, shu_up, shsilu_done, shhid_done = sem("shg_up"), sem("shu_up"), sem("shsilu_done"), sem("shhid_done")
        shd_up, base_done = sem("shd_up"), sem("base_done")
        gathered = [sem(f"gathered{s}") for s in range(NS)]
        xs_up, xs_done, gu_up, ss_done, sh_done = sem("xs_up"), sem("xs_done"), sem("gu_up"), sem("ss_done"), sem("sh_done")
        ht_up, ht_done, y_up, y_done = sem("ht_up"), sem("ht_done"), sem("y_up"), sem("y_done")
        scattered = sem("scattered")
        ld_y = [sem(f"ld_y{b}") for b in range(B)]
        gy_done, o_done, stored = sem("gy_done"), sem("o_done"), sem("stored")
        dve_step, pool_step = sem("dve_step"), sem("pool_step")

        x_v = x.rearrange("(b p t) h -> b p t h", p=P, t=T)
        out_v = out.rearrange("b (p t) h -> b p t h", p=P)
        z_v = z_rows.rearrange("(b p t) w -> b p t w", p=P, t=T)
        y_v = y_rows.rearrange("(b p t) h -> b p t h", p=P, t=T)

        def tiles(buf, b):
            return buf[:, T * b:T * b + T]

        def over(ap, shape):
            return ap.broadcast_to(shape)

        block = ctx.enter_context(nc.Block())

        @block.sync
        def _(sp):
            sp.dma_start(vec_rows[:, :], vecs).then_inc(ld_vec, 16)
            sp.dma_start(tiles(x_in, 0), x_v[0]).then_inc(ld_x[0], 16)
            sp.dma_start(wmod_sb[:, :], wmod).then_inc(ld_wmod, 16)
            sp.dma_start(wqkv_sb[:, :, :], wqkv).then_inc(ld_wqkv, 16)
            sp.dma_start(bv_rows[:, :], bv.partition_broadcast(B)).then_inc(ld_bv, 16)
            for b in range(1, B):
                sp.dma_start(tiles(x_in, b), x_v[b]).then_inc(ld_x[b], 16)
            sp.dma_start(router_sb[:, :], router_w).then_inc(ld_router, 16)
            sp.dma_start(sh_gu_sb[:, :], sh_gu).then_inc(ld_sh_gu, 16)
            sp.dma_start(sh_down_sb[:, :, :], sh_down).then_inc(ld_sh_down, 16)
            sp.dma_start(w_gu_sb[:, :], w_gu).then_inc(ld_gu, 16)
            sp.dma_start(w_down_sb[:, :], w_down).then_inc(ld_down, 16)
            for b in range(B):
                sp.wait_ge(z_done, T * (b + 1))
                sp.wait_ge(w_done, b + 1)
                sp.dma_start(z_v[b], tiles(zw, b)).then_inc(z_stored, 16)
            sp.wait_ge(scattered, 16 * NS)
            for b in range(B):
                sp.dma_start(tiles(y_tok, b), y_v[b]).then_inc(ld_y[b], 16)
            for b in range(B):
                sp.wait_ge(o_done, b + 1)
                sp.dma_start(out_v[b], tiles(o_sb, b)).then_inc(stored, 16)
            sp.wait_ge(stored, 16 * B)
            sp.wait_ge(z_stored, 16 * B)

        @block.gpsimd
        def _(pool):
            small = Steps(pool, pool_step)

            def hot(buf, fill):
                pool.affine_select(out=buf[:, :], in_=buf[:, :], pattern=[[-1, P]], base=0, channel_multiplier=1,
                                   compare_op=ALU.not_equal, fill=fill).then_inc(c_done, 1)

            pool.memset(ident[:, :], 0.0).then_inc(c_set, 1)
            pool.memset(pick_b[:, :, :], 0.0).then_inc(c_set, 1)
            pool.memset(mask_diag[:, :], 0.0).then_inc(c_set, 1)
            pool.memset(before[:, :], 1.0).then_inc(c_set, 1)
            pool.memset(ident_b[:, :], 0.0).then_inc(c_set, 1)
            pool.memset(earlier_e[:, :, :], 1.0).then_inc(c_set, 1)
            pool.wait_ge(c_set, 1)
            hot(ident, 1.0)
            pool.wait_ge(c_set, 6)
            pool.affine_select(out=pick_b[:, :, :], in_=pick_b[:, :, :], pattern=[[-1, B], [0, P]], base=0,
                               channel_multiplier=1, compare_op=ALU.not_equal, fill=1.0).then_inc(c_done, 1)
            hot(mask_diag, LOWEST)
            hot(ident_b, 1.0)
            pool.memset(ones_b[:, :], 1.0).then_inc(c_done, 1)
            pool.affine_select(out=before[:, :], in_=before[:, :], pattern=[[1, P]], base=0, channel_multiplier=-1,
                               compare_op=ALU.is_gt, fill=0.0).then_inc(c_done, 1)
            pool.affine_select(out=earlier_e[:, :, :], in_=earlier_e[:, :, :], pattern=[[1, E], [-1, E]], base=0,
                               channel_multiplier=0, compare_op=ALU.is_gt, fill=0.0).then_inc(c_done, 1)

            def ramp(buf, pattern, base=0, channel=0):
                pool.iota(buf[:, :], pattern=pattern, base=base, channel_multiplier=channel,
                          allow_small_or_imprecise_dtypes=True).then_inc(c_done, 1)

            ramp(iota_p, [[1, P]])
            ramp(iota_e, [[1, E]])
            ramp(iota_e8, [[1, E]], base=-E)
            ramp(iota_s, [[1, NS]])
            ramp(steps_128, [[P, NT]])
            ramp(batch_512, [[L, B], [0, T]])
            ramp(tile_8, [[0, B], [1, T]], base=8)
            ramp(part_4, [[0, 1]], channel=T)
            pool.memset(seen[:, 0, :], 0.0).then_inc(c_done, 1)


            def residual(b):
                pool.wait_ge(ld_x[b], 16)
                pool.wait_ge(bc_done, b + 1)
                pool.tensor_tensor(tiles(x_res, b), tiles(x_in, b), over(bc[:, b, 3:4, :], [P, T, H]),
                                   ALU.add).then_inc(xres_done, 1)

            def shared_down(b):
                pool.wait_ge(bc_done, b + 1)
                pool.wait_ge(ld_sh_down, 16)
                pool.tensor_tensor(sh_down_gb[:, b], sh_down_sb[:, :, :], over(bc[:, b, 0:1, :], [P, IC, H]),
                                   ALU.mult).then_inc(shd_done, 1)

            def carry(b):
                pool.wait_ge(hot_done, b + 1)
                pool.tensor_copy(tiles(onehot_b, b), tiles(onehot, b)).then_inc(hotb_done, 1)
                pool.wait_ge(seen_sum, b + 1)
                if b == 0:
                    pool.wait_ge(c_done, 16)
                else:
                    pool.wait_ge(seen_done, b)
                pool.tensor_tensor(seen[:, b + 1, :], seen[:, b, :], seen_new[:, b, :], ALU.add).then_inc(seen_done, 1)

            def base_rows(b):
                pool.wait_ge(h2_done, T * (b + 1))
                if b >= 1:
                    pool.wait_ge(xb_done, b)
                pool.tensor_tensor(gh2[:, :, :], tiles(h2, b), over(bc[:, b, 0:1, :], [P, T, H]),
                                   ALU.mult).then_inc(gh2_done, 1)
                pool.wait_ge(x1_done, T * (b + 1))
                pool.wait_ge(gh2_done, b + 1)
                pool.tensor_tensor(tiles(xb, b), gh2[:, :, :], tiles(x1, b), ALU.add).then_inc(xb_done, 1)

            def row_hots(b):
                pool.wait_ge(rmod_done, b + 1)
                if b == 0:
                    pool.wait_ge(c_done, 16)
                for n in range(T * b, T * b + T):
                    pool.tensor_scalar(row_hot[:, n, :], iota_p[:, :], rank_mod[:, n:n + 1], None,
                                       ALU.is_equal).then_inc(rowhot_done, 1)

            residual(0)
            for b in range(B):
                if b + 1 < B:
                    residual(b + 1)
                shared_down(b)
                if b >= 1:
                    base_rows(b - 1)
                    carry(b - 1)
                    row_hots(b - 1)
            base_rows(B - 1)
            carry(B - 1)
            pool.wait_ge(gidx_done, 1)
            pool.wait_ge(z_stored, 16 * B)
            for s in range(NS):
                pool.indirect_dma_start(out=zg[:, s, :], out_offset=None, in_=z_rows,
                                        in_offset=bass.IndirectOffsetOnAxis(ap=gather_i[:, s:s + 1], axis=0)
                                        ).then_inc(gathered[s], 16)
            pool.wait_ge(sidx_done, 1)
            for s in range(NS):
                pool.wait_ge(y_done, s + 1)
                pool.indirect_dma_start(out=y_rows, out_offset=bass.IndirectOffsetOnAxis(ap=scatter_i[:, s:s + 1], axis=0),
                                        in_=y_sl[:, s, :], in_offset=None, bounds_check=B * L - 1,
                                        oob_is_err=False).then_inc(scattered, 16)

        @block.scalar
        def _(act):
            def broadcast_rows(b):
                act.wait_ge(row_up, b + 1)
                act.activation(bc[:, b, :, :], M[1][:, :].rearrange("p (j h) -> p j h", j=4), ACT.Copy).then_inc(bc_done, 1)

            def h_rows(b):
                act.wait_ge(nT_up, b + 1)
                act.wait_ge(modc_done, 2)
                act.activation(hT[:, :], M[0][:, :], ACT.Identity, bias=shift_a[:, b:b + 1],
                               scale=scale_a[:, b:b + 1]).then_inc(hT_done, 1)

            def q_rows(b):
                act.wait_ge(q_up, b + 1)
                act.activation(qT[:, :], M[1][:, :], ACT.Identity, bias=bq_h[:, 0:1], scale=1.0 / H).then_inc(qT_done, 1)

            def k_rows(b):
                act.wait_ge(k_up, b + 1)
                act.activation(kT[:, :], M[0][:, :], ACT.Identity, bias=cols[:, 1:2]).then_inc(kT_done, 1)

            def v_rows(b):
                act.wait_ge(v_up, b + 1)
                act.activation(v_sb[:, b % 2], M[1][:, :].rearrange("p (t h) -> p t h", t=T), ACT.Copy).then_inc(v_done, 1)

            def exps(n):
                act.wait_ge(max_done, n + 1)
                if n >= 2:
                    act.wait_ge(pT_up, n - 1)
                act.activation(probs[:, n % 2, :], S[n % 2][:, :], ACT.Exp, bias=neg_max[:, n:n + 1],
                               accum_out=prob_sum[:, n:n + 1]).then_inc(p_done, 1)

            def probs_T(n):
                act.wait_ge(pT_up, n + 1)
                if n >= 2:
                    act.wait_ge(o_up, n - 1)
                act.activation(probsT[:, n % 2, :], PT[n % 2][:, :], ACT.Copy).then_inc(pT_done, 1)

            def xf_rows(b):
                act.wait_ge(zT_up, b + 1)
                act.activation(xfT[:, b, :], M[0][:, :], ACT.Identity, bias=cols[:, 3:4], scale=cols[:, 2:3]).then_inc(xfT_done, 1)

            def score_exp(b):
                act.wait_ge(top_done, b + 1)
                act.activation(tiles(exp_top, b), tiles(top, b), ACT.Exp, scale=-1.0).then_inc(exp_done, 1)

            act.wait_ge(cols_done, 1)
            act.activation(silu_c[:, :], cols[:, 4:8], ACT.Silu).then_inc(silu_done, 1)
            act.wait_ge(cols_done, 2)
            h_rows(0)
            q_rows(0)
            k_rows(0)
            broadcast_rows(0)
            v_rows(0)
            exps(0)
            exps(1)
            for b in range(B):
                n = T * b
                nxt = b + 1 < B
                probs_T(n)
                exps(n + 2)
                probs_T(n + 1)
                exps(n + 3)
                if nxt:
                    h_rows(b + 1)
                probs_T(n + 2)
                if nxt:
                    q_rows(b + 1)
                    k_rows(b + 1)
                    broadcast_rows(b + 1)
                probs_T(n + 3)
                if nxt:
                    v_rows(b + 1)
                    exps(n + T)
                if b >= 1:
                    xf_rows(b - 1)
                if nxt:
                    exps(n + T + 1)
                if b >= 1:
                    score_exp(b - 1)
            xf_rows(B - 1)
            score_exp(B - 1)
            for b in range(B):
                for c in range(IC):
                    k = IC * b + c
                    act.wait_ge(shg_up, k + 1)
                    if b >= 1:
                        act.wait_ge(shhid_done, k - 1)
                    act.activation(sh_silu[:, c, :], S[c][:, :], ACT.Silu).then_inc(shsilu_done, 1)
            for s in range(NS + 1):
                if s < NS:
                    act.wait_ge(gu_up, s + 1)
                    if s >= 2:
                        act.wait_ge(sh_done, s - 1)
                    act.activation(sl_silu[:, s % 2, :], S[s % 2][:, 0:I], ACT.Silu,
                                   scale=zg[:, s, H:H + 1]).then_inc(ss_done, 1)
                if s >= 1:
                    act.wait_ge(ht_up, s)
                    if s >= 3:
                        act.wait_ge(y_up, s - 2)
                    act.activation(sl_hidT[:, (s - 1) % 2], PT[(s - 1) % 2][:, 0:I].rearrange("p (c q) -> p c q", c=IC),
                                   ACT.Copy).then_inc(ht_done, 1)

        @block.vector
        def _(dve):
            small = Steps(dve, dve_step)

            def rsqrt(v, t, r, mv, lo, hi):
                v, t, r = v[:, lo:hi], t[:, lo:hi], r[:, lo:hi]
                small.chain(dve.tensor_scalar(v, mv[:, lo:hi, 1], EPS, None, ALU.add))
                small.chain(dve.tensor_scalar(r.bitcast(I32), v.bitcast(I32), -0.5, RSQRT_MAGIC, ALU.mult, ALU.add))
                for _ in range(3):
                    small.chain(dve.tensor_tensor(t, r, r, ALU.mult))
                    small.chain(dve.scalar_tensor_tensor(out=t, in0=t, scalar=-0.5, in1=v, op0=ALU.mult, op1=ALU.mult))
                    small.chain(dve.scalar_tensor_tensor(out=r, in0=t, scalar=1.5, in1=r, op0=ALU.add, op1=ALU.mult))

            def stats(src, st, mv, st_done, mv_done, n):
                dve.bn_stats(st[:, n, :], src[:, n, :]).then_inc(st_done, 1)

            def aggregate(st, mv, st_done, mv_done, n):
                dve.wait_ge(st_done, n + 1)
                dve.bn_aggr(mv[:, n, :], st[:, n, :]).then_inc(mv_done, 1)

            def norm1_stats(b):
                dve.wait_ge(ld_x[b], 16)
                for n in range(T * b, T * b + T):
                    stats(x_in, st1, mv1, st1_done, mv1_done, n)
                for n in range(T * b, T * b + T):
                    aggregate(st1, mv1, st1_done, mv1_done, n)
                dve.wait_ge(mv1_done, T * (b + 1))
                rsqrt(v1, t1, r1, mv1, T * b, T * b + T)

            def norm1(b):
                if b >= 1:
                    dve.wait_ge(nT_up, b)
                for t in range(T):
                    n = T * b + t
                    dve.tensor_scalar(normed[:, t, :], x_in[:, n, :], mv1[:, n, 0:1], r1[:, n:n + 1],
                                      ALU.subtract, ALU.mult).then_inc(norm_done, 1)

            def gated_v_weights(b):
                dve.wait_ge(ga_up, b + 1)
                dve.tensor_tensor(wv_ga[:, b, :], wqkv_sb[:, 2, :], M[0][:, 0:H], ALU.mult).then_inc(wv_done, 1)

            def score_max(n):
                dve.wait_ge(s_up, n + 1)
                dve.tensor_reduce(neg_max[:, n:n + 1], S[n % 2][:, :], AX_X, ALU.max, negate=True).then_inc(max_done, 1)

            def attention_out(n):
                dve.wait_ge(p_done, n + 1)
                dve.reciprocal(prob_inv[:, n:n + 1], prob_sum[:, n:n + 1]).then_inc(inv_done, 1)
                dve.wait_ge(inv_done, n + 1)
                dve.wait_ge(xres_done, n // T + 1)
                dve.wait_ge(o_up, n + 1)
                dve.scalar_tensor_tensor(out=x1[:, n, :], in0=O[n % 2][:, 0:H], scalar=prob_inv[:, n:n + 1],
                                         in1=x_res[:, n, :], op0=ALU.mult, op1=ALU.add).then_inc(x1_done, 1)

            def norm2(b):
                lo, hi = T * b, T * b + T
                for n in range(lo, hi):
                    dve.wait_ge(x1_done, n + 1)
                    stats(x1, st2, mv2, st2_done, mv2_done, n)
                for n in range(lo, hi):
                    aggregate(st2, mv2, st2_done, mv2_done, n)
                dve.wait_ge(mv2_done, hi)
                rsqrt(v2, t2, r2, mv2, lo, hi)
                dve.wait_ge(bc_done, b + 1)
                for n in range(lo, hi):
                    dve.scalar_tensor_tensor(out=h2u[:, n, :], in0=x1[:, n, :], scalar=mv2[:, n, 0:1], in1=bc[:, b, 2, :],
                                             op0=ALU.subtract, op1=ALU.mult).then_inc(h2u_done, 1)
                for n in range(lo, hi):
                    dve.wait_ge(h2u_done, n + 1)
                    dve.scalar_tensor_tensor(out=h2[:, n, :], in0=h2u[:, n, :], scalar=r2[:, n:n + 1], in1=bc[:, b, 1, :],
                                             op0=ALU.mult, op1=ALU.add).then_inc(h2_done, 1)

            def norm3(b):
                lo, hi = T * b, T * b + T
                for n in range(lo, hi):
                    dve.wait_ge(h2_done, n + 1)
                    stats(h2, st3, mv3, st3_done, mv3_done, n)
                for n in range(lo, hi):
                    aggregate(st3, mv3, st3_done, mv3_done, n)
                dve.wait_ge(mv3_done, hi)
                rsqrt(v3, t3, r3, mv3, lo, hi)
                for n in range(lo, hi):
                    dve.tensor_scalar(zw[:, n, 0:H], h2[:, n, :], mv3[:, n, 0:1], r3[:, n:n + 1],
                                      ALU.subtract, ALU.mult).then_inc(z_done, 1)

            def route(b):
                lg = M[1][:, 0:T * E].rearrange("p (t e) -> p t e", t=T)
                dve.wait_ge(lg_up, b + 1)
                dve.tensor_reduce(tiles(top, b), lg, AX_X, ALU.max).then_inc(top_done, 1)
                dve.wait_ge(top_done, b + 1)
                if b == 0:
                    dve.wait_ge(c_done, 16)
                dve.tensor_tensor(tiles(is_top, b), lg, over(tiles(top, b).unsqueeze(2), [P, T, E]),
                                  ALU.is_equal).then_inc(lg_read, 1)
                dve.wait_ge(lg_read, b + 1)
                small.chain(dve.scalar_tensor_tensor(out=tiles(cand, b), in0=tiles(is_top, b), scalar=-float(E),
                                                     in1=over(iota_e[:, :].unsqueeze(1), [P, T, E]), op0=ALU.mult, op1=ALU.add))
                small.chain(dve.tensor_reduce(tiles(first, b), tiles(cand, b), AX_X, ALU.min))
                dve.tensor_tensor(tiles(onehot, b), over(iota_e8[:, :].unsqueeze(1), [P, T, E]),
                                  over(tiles(first, b).unsqueeze(2), [P, T, E]), ALU.is_equal).then_inc(hot_done, 1)
                dve.wait_ge(hot_done, b + 1)
                dve.tensor_reduce(seen_new[:, b, :], tiles(onehot, b).rearrange("p t e -> p e t"), AX_X,
                                  ALU.add).then_inc(seen_sum, 1)
                dve.wait_ge(exp_done, b + 1)
                small.chain(dve.tensor_scalar(tiles(exp_top1, b), tiles(exp_top, b), 1.0, None, ALU.add))
                dve.reciprocal(tiles(zw, b)[:, :, H], tiles(exp_top1, b)).then_inc(w_done, 1)

            def ranks(b):
                dve.wait_ge(rank_up, b + 1)
                dve.tensor_tensor(tiles(rank_of, b), tiles(onehot, b), M[1][:, 64:64 + T * E].rearrange("p (t e) -> p t e", t=T),
                                  ALU.mult).then_inc(rank_read, 1)
                dve.wait_ge(rank_read, b + 1)
                small.chain(dve.tensor_reduce(tiles(rank, b), tiles(rank_of, b), AX_X, ALU.add))
                small.chain(dve.tensor_copy(tiles(rank_i, b), tiles(rank, b)))
                small.chain(dve.tensor_scalar(tiles(rank_div_i, b), tiles(rank_i, b), 7, None, ALU.arith_shift_right))
                small.chain(dve.tensor_copy(tiles(rank_div, b), tiles(rank_div_i, b)))
                dve.scalar_tensor_tensor(out=tiles(rank_mod, b), in0=tiles(rank_div, b), scalar=-float(P), in1=tiles(rank, b),
                                         op0=ALU.mult, op1=ALU.add).then_inc(rmod_done, 1)

            def slot_tables():
                dve.wait_ge(cnt_up, 1)
                dve.tensor_copy(count[:, :], M[1][:, 128:128 + E]).then_inc(cnt_read, 1)
                dve.wait_ge(cnt_read, 1)
                small.chain(dve.tensor_tensor(count_over[:, :, :], over(count[:, :].unsqueeze(2), [P, E, NT]),
                                              over(steps_128[:, :].unsqueeze(1), [P, E, NT]), ALU.is_gt))
                small.chain(dve.tensor_reduce(slots_of[:, :], count_over[:, :, :], AX_X, ALU.add))
                small.chain(dve.tensor_tensor(slots_before[:, :, :], over(slots_of[:, :].unsqueeze(1), [P, E, E]),
                                              earlier_e[:, :, :], ALU.mult))
                small.chain(dve.tensor_reduce(slot0[:, :], slots_before[:, :, :], AX_X, ALU.add))
                small.chain(dve.tensor_tensor(slot_pick[:, :, :], onehot[:, :, :], over(slot0[:, :].unsqueeze(1), [P, NT, E]), ALU.mult))
                small.chain(dve.tensor_reduce(slot_first[:, :], slot_pick[:, :, :], AX_X, ALU.add))
                small.chain(dve.tensor_tensor(slot[:, :], slot_first[:, :], rank_div[:, :], ALU.add))
                small.chain(dve.tensor_tensor(slot_diff[:, :, :], over(slot[:, :].unsqueeze(2), [P, NT, NS]),
                                              over(iota_s[:, :].unsqueeze(1), [P, NT, NS]), ALU.subtract))
                for j, part in enumerate((tile_8, batch_512)):
                    dve.scalar_tensor_tensor(out=slot_val[:, :, j, :], in0=slot_diff[:, :, :], scalar=0.0,
                                             in1=over(part[:, :].unsqueeze(2), [P, NT, NS]), op0=ALU.is_equal,
                                             op1=ALU.mult).then_inc(sval_done, 1)
                dve.tensor_scalar(slot_val[:, :, 2, :], slot_diff[:, :, :], 0.0, part_4[:, 0:1], ALU.is_equal,
                                  ALU.mult).then_inc(sval_done, 1)
                small.chain(dve.tensor_tensor(slot_end[:, :], slot0[:, :], slots_of[:, :], ALU.add))
                small.chain(dve.tensor_tensor(slot_past[:, :, :], over(slot_end[:, :].unsqueeze(1), [P, NS, E]),
                                              over(iota_s[:, :].unsqueeze(2), [P, NS, E]), ALU.is_le))
                small.chain(dve.tensor_reduce(slot_exp[:, :], slot_past[:, :, :], AX_X, ALU.add))
                dve.tensor_scalar(slot_exp_i[:, :], slot_exp[:, :], float(E - 1), None, ALU.min).then_inc(sexp_done, 1)

            def token_tables():
                dve.wait_ge(table_up, 1)
                dve.tensor_copy(table[:, :, :], O[0][:, 0:3 * NS].rearrange("p (j s) -> p j s", j=3)).then_inc(table_read, 1)
                dve.wait_ge(table_read, 1)
                small.chain(dve.scalar_tensor_tensor(out=token_ab[:, :], in0=table[:, 0, :], scalar=-8.0, in1=table[:, 1, :],
                                                     op0=ALU.add, op1=ALU.add))
                small.chain(dve.tensor_tensor(token[:, :], token_ab[:, :], table[:, 2, :], ALU.add))
                dve.tensor_scalar(gather_i[:, :], token[:, :], 0.0, None, ALU.max).then_inc(gidx_done, 1)
                small.chain(dve.tensor_scalar(no_token[:, :], table[:, 0, :], 8.0, SKIP, ALU.is_lt, ALU.mult))
                dve.tensor_tensor(scatter_i[:, :], no_token[:, :], token[:, :], ALU.add).then_inc(sidx_done, 1)

            dve.wait_ge(vec_up, 1)
            dve.tensor_copy(cols[:, :], M[0][:, 0:8]).then_inc(cols_done, 1)
            dve.wait_ge(cols_done, 1)
            dve.tensor_scalar(bq_h[:, :], cols[:, 0:1], 1.0 / H, None, ALU.mult).then_inc(cols_done, 1)
            norm1_stats(0)
            norm1(0)
            dve.wait_ge(modc_up, 1)
            dve.tensor_copy(shift_a[:, :], M[1][:, 0:B]).then_inc(modc_done, 1)
            dve.tensor_scalar(scale_a[:, :], M[1][:, B:2 * B], 1.0, None, ALU.add).then_inc(modc_done, 1)
            dve.wait_ge(modr_up, 1)
            dve.tensor_copy(mod_raw[:, :, :], PT[0][0:B, :].rearrange("p (j h) -> p j h", j=4)).then_inc(modr_raw, 1)
            dve.wait_ge(modr_raw, 1)
            gates = mod_raw[:, 0:4:3, :]
            small.then(dve.tensor_scalar(gate_sign[:, :, :], gates, 0.0, -0.5, ALU.is_ge, ALU.add))
            small.chain(dve.scalar_tensor_tensor(out=gate_abs[:, :, :], in0=gates, scalar=-1.0, in1=gates, op0=ALU.mult, op1=ALU.max))
            small.chain(dve.scalar_tensor_tensor(out=gate_half[:, :, :], in0=gate_abs[:, :, :], scalar=0.25, in1=gate_sign[:, :, :],
                                                 op0=ALU.max, op1=ALU.mult))
            dve.tensor_scalar(mod_rows[:, 0:2, :], gate_half[:, :, :], 2.0, None, ALU.mult).then_inc(modr_done, 1)
            dve.tensor_copy(mod_rows[:, 2, :], mod_raw[:, 1, :]).then_inc(modr_done, 1)
            dve.tensor_scalar(mod_rows[:, 3, :], mod_raw[:, 2, :], 1.0, None, ALU.add).then_inc(modr_done, 1)
            dve.wait_ge(ld_bv, 16)
            dve.wait_ge(modr_done, 1)
            dve.tensor_tensor(mod_rows[:, 4, :], mod_rows[:, 0, :], bv_rows[:, :], ALU.mult).then_inc(modr_done, 1)
            dve.wait_ge(ld_wqkv, 16)
            gated_v_weights(0)
            score_max(0)
            score_max(1)
            for b in range(B):
                n = T * b
                nxt = b + 1 < B
                score_max(n + 2)
                if nxt:
                    norm1_stats(b + 1)
                    norm1(b + 1)
                score_max(n + 3)
                attention_out(n)
                if b >= 1:
                    norm2(b - 1)
                attention_out(n + 1)
                if nxt:
                    gated_v_weights(b + 1)
                attention_out(n + 2)
                attention_out(n + 3)
                if nxt:
                    score_max(n + T)
                if b >= 1:
                    norm3(b - 1)
                if nxt:
                    score_max(n + T + 1)
                if b >= 1:
                    route(b - 1)
                    ranks(b - 1)
            norm2(B - 1)
            norm3(B - 1)
            route(B - 1)
            ranks(B - 1)
            for n in range(T * (B - 1), NT):
                dve.wait_ge(rmod_done, B)
                dve.tensor_scalar(row_hot[:, n, :], iota_p[:, :], rank_mod[:, n:n + 1], None, ALU.is_equal).then_inc(rowhot_done, 1)
            slot_tables()

            def shared_hidden(b):
                for c in range(IC):
                    k = IC * b + c
                    dve.wait_ge(shsilu_done, k + 1)
                    dve.wait_ge(shu_up, k + 1)
                    if b >= 1:
                        dve.wait_ge(shd_up, b)
                    dve.tensor_tensor(sh_hid[:, c, :], sh_silu[:, c, :], PT[c][:, :], ALU.mult).then_inc(shhid_done, 1)

            def shared_out(b):
                dve.wait_ge(shd_up, b + 1)
                dve.wait_ge(xb_done, b + 1)
                dve.tensor_tensor(tiles(base, b), O[1][:, :].rearrange("p (t h) -> p t h", t=T), tiles(xb, b),
                                  ALU.add).then_inc(base_done, 1)

            token_tables()
            for b in range(B):
                shared_hidden(b)
                shared_out(b)
            for s in range(NS + 2):
                if s < NS:
                    dve.wait_ge(xs_up, s + 1)
                    if s >= 2:
                        dve.wait_ge(gu_up, s - 1)
                    dve.tensor_scalar(xsT[:, s % 2, :], M[s % 2][:, 0:P], cols[:, 2:3], cols[:, 3:4], ALU.mult,
                                      ALU.add).then_inc(xs_done, 1)
                if 1 <= s <= NS:
                    k = s - 1
                    dve.wait_ge(ss_done, k + 1)
                    if k >= 2:
                        dve.wait_ge(ht_up, k - 1)
                    dve.scalar_tensor_tensor(out=sl_hid[:, k % 2, :], in0=S[k % 2][:, I:2 * I], scalar=zg[:, k, H:H + 1],
                                             in1=sl_silu[:, k % 2, :], op0=ALU.mult, op1=ALU.mult).then_inc(sh_done, 1)
                if s >= 2:
                    k = s - 2
                    dve.wait_ge(y_up, k + 1)
                    dve.tensor_copy(y_sl[:, k, :], O[k % 2][:, 0:H]).then_inc(y_done, 1)
            for b in range(B):
                dve.wait_ge(ld_y[b], 16)
                dve.tensor_tensor(tiles(gy, b), tiles(y_tok, b), over(bc[:, b, 0:1, :], [P, T, H]), ALU.mult).then_inc(gy_done, 1)
                dve.wait_ge(gy_done, b + 1)
                dve.tensor_tensor(tiles(o_sb, b), tiles(gy, b), tiles(base, b), ALU.add).then_inc(o_done, 1)

        @block.tensor
        def _(pe):
            def transposes(dst, src_of, count):
                for t in range(count):
                    last = pe.transpose(dst[:, t * P:(t + 1) * P], src_of(t), ident[:, :])
                return last

            def rows_T(b):
                pe.wait_ge(norm_done, T * (b + 1))
                if b >= 3:
                    pe.wait_ge(xfT_done, b - 2)
                elif b >= 1:
                    pe.wait_ge(wv_done, b)
                else:
                    pe.wait_ge(cols_done, 1)
                transposes(M[0], lambda t: normed[:, t, :], T).then_inc(nT_up, 1)

            def q_product(b):
                pe.wait_ge(hT_done, b + 1)
                if b >= 3:
                    pe.wait_ge(rank_read, b - 2)
                elif b >= 1:
                    pe.wait_ge(v_done, b)
                else:
                    pe.wait_ge(modc_done, 2)
                pe.matmul(M[1][:, :], wqkv_sb[:, 0, :], hT[:, :], start=True, stop=True).then_inc(q_up, 1)

            def k_product(b):
                pe.matmul(M[0][:, :], wqkv_sb[:, 1, :], hT[:, :], start=True, stop=True).then_inc(k_up, 1)

            def broadcasts(b):
                if b == 0:
                    pe.wait_ge(modr_done, 4)
                    pe.wait_ge(c_done, 16)
                pe.wait_ge(qT_done, b + 1)
                pe.matmul(M[1][:, :], pick_b[:, b, :], mod_rows[:, 1:5, :], start=True, stop=True).then_inc(row_up, 1)
                pe.wait_ge(kT_done, b + 1)
                pe.matmul(M[0][:, 0:H], pick_b[:, b, :], mod_rows[:, 0, :], start=True, stop=True).then_inc(ga_up, 1)

            def v_product(b):
                pe.wait_ge(wv_done, b + 1)
                pe.wait_ge(bc_done, b + 1)
                for t in range(T):
                    last = pe.matmul(M[1][:, t * H:(t + 1) * H], hT[:, t * P:(t + 1) * P], wv_ga[:, b, :], start=True, stop=True)
                last.then_inc(v_up, 1)

            def scores(n):
                b, t = n // T, n % T
                if t == 0:
                    pe.wait_ge(kT_done, b + 1)
                    pe.wait_ge(qT_done, b + 1)
                if n == 0:
                    pe.wait_ge(c_done, 4)
                if n >= 2:
                    pe.wait_ge(p_done, n - 1)
                pe.matmul(S[n % 2][:, :], qT[:, t * P:(t + 1) * P], kT[:, :], start=True, stop=False)
                pe.matmul(S[n % 2][:, t * P:(t + 1) * P], ident_b[:, :], mask_diag[:, :], start=False, stop=True).then_inc(s_up, 1)

            def probs_up(n):
                pe.wait_ge(p_done, n + 1)
                if n >= 2:
                    pe.wait_ge(pT_done, n - 1)
                transposes(PT[n % 2], lambda k: probs[:, n % 2, k * P:(k + 1) * P], T).then_inc(pT_up, 1)

            def attend(n):
                pe.wait_ge(pT_done, n + 1)
                if n % T == 0:
                    pe.wait_ge(v_done, n // T + 1)
                if n >= 2:
                    pe.wait_ge(x1_done, n - 1)
                for k in range(T):
                    last = pe.matmul(O[n % 2][:, 0:H], probsT[:, n % 2, k * P:(k + 1) * P], v_sb[:, n // T % 2, k, :], start=(k == 0), stop=(k == T - 1))
                last.then_inc(o_up, 1)

            def z_T(b):
                pe.wait_ge(z_done, T * (b + 1))
                if b + 2 < B:
                    pe.wait_ge(wv_done, b + 3)
                elif b >= 1:
                    pe.wait_ge(xfT_done, b)
                transposes(M[0], lambda t: zw[:, T * b + t, 0:H], T).then_inc(zT_up, 1)

            def logits(b):
                pe.wait_ge(xfT_done, b + 1)
                if b == 0:
                    pe.wait_ge(ld_router, 16)
                if b + 2 < B:
                    pe.wait_ge(v_done, b + 3)
                elif b >= 1:
                    pe.wait_ge(rank_read, b)
                for t in range(T):
                    last = pe.matmul(M[1][:, t * E:(t + 1) * E], xfT[:, b, t * P:(t + 1) * P], router_sb[:, :], start=True, stop=True)
                last.then_inc(lg_up, 1)

            def rank_product(b):
                pe.wait_ge(hotb_done, b + 1)
                pe.wait_ge(exp_done, b + 1)
                pe.wait_ge(lg_read, b + 1)
                if b >= 1:
                    pe.wait_ge(seen_done, b)
                r = M[1][:, 64:64 + T * E].rearrange("p (t e) -> p t e", t=T)
                pe.matmul(r, before[:, :], tiles(onehot_b, b), start=True, stop=False)
                for t in range(T - 1):
                    pe.matmul(r[:, t + 1:T, :], ones_b[:, :], over(onehot_b[:, T * b + t:T * b + t + 1, :], [P, T - 1 - t, E]),
                              start=False, stop=False)
                pe.matmul(r, ones_b[:, :], over(seen[:, b:b + 1, :], [P, T, E]), start=False, stop=True).then_inc(rank_up, 1)

            def shared_in(b):
                if b == 0:
                    pe.wait_ge(ld_sh_gu, 16)
                for c in range(IC):
                    k = IC * b + c
                    if b >= 1:
                        pe.wait_ge(shsilu_done, k - 1)
                    else:
                        pe.wait_ge(p_done, NT)
                    pe.matmul(S[c][:, :], sh_gu_sb[:, c * P:(c + 1) * P], xfT[:, b, :], start=True, stop=True).then_inc(shg_up, 1)
                    if b >= 1:
                        pe.wait_ge(shhid_done, k - 1)
                    else:
                        pe.wait_ge(pT_done, NT)
                    pe.matmul(PT[c][:, :], sh_gu_sb[:, I + c * P:I + (c + 1) * P], xfT[:, b, :], start=True, stop=True).then_inc(shu_up, 1)

            def shared_out(b):
                pe.wait_ge(shhid_done, IC * (b + 1))
                pe.wait_ge(shd_done, b + 1)
                if b >= 1:
                    pe.wait_ge(base_done, b)
                else:
                    pe.wait_ge(x1_done, NT)
                for t in range(T):
                    for c in range(IC):
                        last = pe.matmul(O[1][:, t * H:(t + 1) * H], sh_hid[:, c, t * P:(t + 1) * P], sh_down_gb[:, b, c, :],
                                         start=(c == 0), stop=(c == IC - 1))
                last.then_inc(shd_up, 1)

            pe.wait_ge(ld_vec, 16)
            pe.wait_ge(c_done, 1)
            pe.transpose(M[0][:, 0:8], vec_rows[:, :], ident[0:8, 0:8]).then_inc(vec_up, 1)
            pe.wait_ge(silu_done, 1)
            pe.wait_ge(ld_wmod, 16)
            for j in range(2):
                last = pe.matmul(M[1][:, j * B:(j + 1) * B], wmod_sb[:, j * H:(j + 1) * H], silu_c[:, :], start=True, stop=True)
            last.then_inc(modc_up, 1)
            pe.matmul(PT[0][0:B, :], silu_c[:, :], wmod_sb[:, 2 * H:6 * H], start=True, stop=True).then_inc(modr_up, 1)
            rows_T(0)
            pe.wait_ge(ld_wqkv, 16)
            q_product(0)
            k_product(0)
            broadcasts(0)
            v_product(0)
            scores(0)
            scores(1)
            for b in range(B):
                n = T * b
                nxt = b + 1 < B
                probs_up(n)
                scores(n + 2)
                if b == 0:
                    pe.wait_ge(modr_raw, 1)
                attend(n)
                probs_up(n + 1)
                scores(n + 3)
                attend(n + 1)
                if nxt:
                    rows_T(b + 1)
                probs_up(n + 2)
                attend(n + 2)
                if nxt:
                    q_product(b + 1)
                    k_product(b + 1)
                probs_up(n + 3)
                if nxt:
                    broadcasts(b + 1)
                    v_product(b + 1)
                attend(n + 3)
                if nxt:
                    scores(n + T)
                if b >= 1:
                    z_T(b - 1)
                if nxt:
                    scores(n + T + 1)
                if b >= 1:
                    logits(b - 1)
                    rank_product(b - 1)
            shared_in(0)
            z_T(B - 1)
            logits(B - 1)
            rank_product(B - 1)
            pe.wait_ge(seen_done, B)
            pe.wait_ge(rank_read, B)
            pe.matmul(M[1][:, 128:128 + E], ones_b[:, :], seen[:, B, :], start=True, stop=True, skip_group_check=True).then_inc(cnt_up, 1)
            pe.wait_ge(sval_done, 3)
            pe.wait_ge(rowhot_done, NT)
            pe.wait_ge(x1_done, NT)
            for n in range(NT):
                last = pe.matmul(O[0][:, 0:3 * NS], row_hot[:, n, :], slot_val[:, n, :, :].rearrange("p j s -> p (j s)"),
                                 start=(n == 0), stop=(n == NT - 1))
            last.then_inc(table_up, 1)
            shared_out(0)
            for b in range(1, B):
                shared_in(b)
                shared_out(b)

            pe.wait_ge(sexp_done, 1)
            pe.wait_ge(ld_gu, 16)
            pe.wait_ge(ld_down, 16)
            expert = [None] * NS

            def slot_T(s):
                pe.wait_ge(gathered[s], 16)
                if s >= 2:
                    pe.wait_ge(xs_done, s - 1)
                else:
                    pe.wait_ge(cnt_read, 1)
                pe.transpose(M[s % 2][:, 0:P], zg[:, s, 0:H], ident[:, :]).then_inc(xs_up, 1)

            def slot_in(s):
                expert[s] = pe.value_load(slot_exp_i[0:1, s:s + 1], min_val=0, max_val=E - 1)
                pe.wait_ge(xs_done, s + 1)
                if s >= 2:
                    pe.wait_ge(sh_done, s - 1)
                else:
                    pe.wait_ge(shsilu_done, IC * B)
                pe.matmul(S[s % 2][:, :], xsT[:, s % 2, :], w_gu_sb[:, bass.ds(expert[s] * (2 * I), 2 * I)],
                          start=True, stop=True).then_inc(gu_up, 1)

            def slot_hid_T(s):
                pe.wait_ge(sh_done, s + 1)
                if s >= 2:
                    pe.wait_ge(ht_done, s - 1)
                transposes(PT[s % 2], lambda c: sl_hid[:, s % 2, c * P:(c + 1) * P], IC).then_inc(ht_up, 1)

            def slot_out(s):
                pe.wait_ge(ht_done, s + 1)
                if s >= 2:
                    pe.wait_ge(y_done, s - 1)
                else:
                    pe.wait_ge(base_done, B)
                for c in range(IC):
                    last = pe.matmul(O[s % 2][:, 0:H], sl_hidT[:, s % 2, c, :],
                                     w_down_sb[:, bass.ds(expert[s] * (IC * H) + c * H, H)], start=(c == 0), stop=(c == IC - 1))
                last.then_inc(y_up, 1)

            slot_T(0)
            for s in range(NS + 2):
                if s + 1 < NS:
                    slot_T(s + 1)
                if s < NS:
                    slot_in(s)
                if s >= 2:
                    slot_out(s - 2)
                if 1 <= s <= NS:
                    slot_hid_T(s - 1)


def kernel(**inputs):
    import numpy as np
    import concourse.bacc as bacc
    from concourse.bass_utils import run_bass_kernel_spmd

    a = {k.removeprefix("L0_"): np.asarray(v) for k, v in inputs.items()}
    side_by_side = lambda g, u, axis: np.concatenate([g, u], axis=axis)
    arrays = {
        "x": a["attn_x"].reshape(B * L, H),
        "vecs": np.concatenate([np.stack([a["attn_bq"], a["attn_bk"], a["ffn_ln_w"], a["ffn_ln_b"]]), a["c"]]),
        "bv": a["attn_bv"],
        "wmod": a["wmod"],
        "wqkv": np.stack([a["attn_Wq"].T, a["attn_Wk"].T, a["attn_Wv"].T], axis=1),
        "router_w": a["ffn_router_w"],
        "w_gu": side_by_side(a["ffn_gate_w"], a["ffn_up_w"], 2).transpose(1, 0, 2).reshape(H, E * 2 * I),
        "w_down": a["ffn_down_w"].reshape(E, IC, P, H).transpose(2, 0, 1, 3).reshape(P, E * IC * H),
        "sh_gu": side_by_side(a["ffn_sh_gate"], a["ffn_sh_up"], 1),
        "sh_down": a["ffn_sh_down"].reshape(IC, P, H).transpose(1, 0, 2),
    }
    arrays = {f"in_{k}": np.ascontiguousarray(v) for k, v in arrays.items()}
    nc = bacc.Bacc("TRN2", target_bir_lowering=False, num_devices=1)
    args = [nc.dram_tensor(k, v.shape, mybir.dt.from_np(v.dtype), kind="ExternalInput").ap() for k, v in arrays.items()]
    out = nc.dram_tensor("out_0", (B, L, H), F32, kind="ExternalOutput").ap()
    adaln_block(nc, *args, out)
    r = run_bass_kernel_spmd(nc, [arrays], core_ids=[0])
    return r.results[0]["out_0"]
```

```python
from contextlib import ExitStack

import concourse.bass as bass
from concourse import mybir

F32 = mybir.dt.float32
BF16 = mybir.dt.bfloat16
F32R = mybir.dt.float32r
I32 = mybir.dt.int32
ALU = mybir.AluOpType
ACT = mybir.ActivationFunctionType
AX_X = mybir.AxisListType.X

P = 128
B = 4
L = 512
H = 128
T = L // P
NT = B * T
E = 8
I = 256
IC = I // P
NS = NT + E - 1
ZW = 2 * H + 1
NPAD = NS * P - B * L
EPS = 1e-5
LOWEST = -3.3895313892515355e38
RSQRT_MAGIC = float(0x5F3759DF)
RING = 10
ROUND = 1.5 * (1 << 23)


class Steps:

    def __init__(self, eng, sem):
        self.eng, self.sem, self.count = eng, sem, 0

    def then(self, instruction):
        instruction.then_inc(self.sem, 1)
        self.count += 1

    def done(self):
        self.eng.wait_ge(self.sem, self.count)

    def chain(self, instruction):
        self.then(instruction)
        self.done()


def adaln_block(nc, x, vecs, bv, wmod, wqkv, router_w, w_gu, w_down, sh_gu, sh_down, out):
    z_rows = nc.dram_tensor("z_rows", [B * L, ZW], F32).ap()

    ctx = ExitStack()
    with ctx:
        def sb(name, shape, dt=F32):
            return ctx.enter_context(nc.sbuf_tensor(name, shape, dt))

        def bank(name):
            return ctx.enter_context(nc.psum_tensor(name, [P, 512], F32))

        def sem(name):
            return ctx.enter_context(nc.semaphore(name))

        xs = sb("xs", [P, NT, H])
        vec_rows = sb("vec_rows", [8, H])
        bv_rows = sb("bv_rows", [B, H])
        wmod_sb = sb("wmod_sb", [P, 6 * H])
        wqkv_sb = sb("wqkv_sb", [P, 3, H])
        router_sb = sb("router_sb", [P, E])
        w_gu_sb = sb("w_gu_sb", [P, E * 2 * I])
        w_gu_hi = sb("w_gu_hi", [P, E * 2 * I], F32R)
        w_gu_lo = sb("w_gu_lo", [P, E * 2 * I], F32R)
        w_down_sb = sb("w_down_sb", [P, E * IC * H])
        sh_gu_sb = sb("sh_gu_sb", [P, 2 * I])
        sh_gu_hi = sb("sh_gu_hi", [P, 2 * I], F32R)
        sh_gu_lo = sb("sh_gu_lo", [P, 2 * I], F32R)
        sh_down_sb = sb("sh_down_sb", [P, IC, H])
        ident = sb("ident", [P, P])
        ident_b = sb("ident_b", [P, P], BF16)
        mask_diag = sb("mask_diag", [P, P], BF16)
        not_before = sb("not_before", [P, P], BF16)
        ones_b = sb("ones_b", [P, P], BF16)
        iota_p = sb("iota_p", [P, P], BF16)
        iota_e = sb("iota_e", [P, E])
        iota_e8 = sb("iota_e8", [P, E])
        iota_s = sb("iota_s", [P, NS])
        pad_base = sb("pad_base", [P, NS])
        same_e = sb("same_e", [P, E, NT])
        steps_128 = sb("steps_128", [P, NT])
        earlier_e = sb("earlier_e", [P, E, E])
        batch_512 = sb("batch_512", [P, NT])
        tile_8 = sb("tile_8", [P, NT])
        part_4 = sb("part_4", [P, 1])
        pick_b = sb("pick_b", [B, B, P])
        cols = sb("cols", [P, 8])
        bq_h = sb("bq_h", [P, 1])
        silu_c = sb("silu_c", [P, B])
        shift_a = sb("shift_a", [P, B])
        scale_a = sb("scale_a", [P, B])
        mod_raw = sb("mod_raw", [B, 4, H])
        gate_sign = sb("gate_sign", [B, 2, H])
        gate_abs = sb("gate_abs", [B, 2, H])
        gate_half = sb("gate_half", [B, 2, H])
        mod_rows = sb("mod_rows", [B, 5, H])
        bc = sb("bc", [P, B, 4, H])
        wv_ga = sb("wv_ga", [P, B, H])
        sh_down_gb = sb("sh_down_gb", [P, B, IC, H])
        st1 = sb("st1", [P, NT, 6])
        mv1 = sb("mv1", [P, NT, 2])
        v1 = sb("v1", [P, NT])
        t1 = sb("t1", [P, NT])
        r1 = sb("r1", [P, NT])
        nmr1 = sb("nmr1", [P, NT])
        normed = sb("normed", [P, T, H])
        hT = sb("hT", [P, L])
        qT = sb("qT", [P, L])
        kT = sb("kT", [P, L])
        v_sb = sb("v_sb", [P, 2, T, H])
        neg_max = sb("neg_max", [P, NT])
        probs = sb("probs", [P, 2, L])
        prob_sum = sb("prob_sum", [P, NT])
        prob_inv = sb("prob_inv", [P, NT])
        probsT = sb("probsT", [P, 2, L])
        st2 = sb("st2", [P, NT, 6])
        mv2 = sb("mv2", [P, NT, 2])
        v2 = sb("v2", [P, NT])
        t2 = sb("t2", [P, NT])
        r2 = sb("r2", [P, NT])
        h2u = sb("h2u", [P, T, H])
        h2 = sb("h2", [P, T, H])
        st3 = sb("st3", [P, NT, 6])
        mv3 = sb("mv3", [P, NT, 2])
        v3 = sb("v3", [P, NT])
        t3 = sb("t3", [P, NT])
        r3 = sb("r3", [P, NT])
        zw = sb("zw", [P, NT, ZW])
        gh2 = sb("gh2", [P, T, H])
        xfT = sb("xfT", [P, L])
        xf_hi = sb("xf_hi", [P, B, L], F32R)
        xf_lo = sb("xf_lo", [P, B, L], F32R)
        lg = sb("lg", [P, NT, E])
        top = sb("top", [P, NT])
        tanh_top = sb("tanh_top", [P, NT])
        is_top = sb("is_top", [P, NT, E])
        cand = sb("cand", [P, NT, E])
        first = sb("first", [P, NT])
        onehot = sb("onehot", [P, E, NT], BF16)
        seen = sb("seen", [P, E, NT], BF16)
        rank_of = sb("rank_of", [P, NT, E])
        rank = sb("rank", [P, NT])
        rank_128 = sb("rank_128", [P, NT])
        rank_div = sb("rank_div", [P, NT])
        rank_mod = sb("rank_mod", [P, NT])
        row_hot = sb("row_hot", [P, NT, P], BF16)
        count = sb("count", [P, E])
        count_over = sb("count_over", [P, E, NT])
        slots_of = sb("slots_of", [P, E])
        slots_before = sb("slots_before", [P, E, E])
        slot0 = sb("slot0", [P, E])
        slot_end = sb("slot_end", [P, E])
        slot_pick = sb("slot_pick", [P, NT, E])
        slot_first = sb("slot_first", [P, NT])
        slot = sb("slot", [P, NT])
        slot_diff = sb("slot_diff", [P, NT, NS])
        slot_val = sb("slot_val", [P, NT, 3, NS], BF16)
        table = sb("table", [P, 3, NS])
        token_ab = sb("token_ab", [P, NS])
        token = sb("token", [P, NS])
        pad_row = sb("pad_row", [P, NS])
        pad_or_0 = sb("pad_or_0", [P, NS])
        gather_i = sb("gather_i", [P, NS], I32)
        scatter_i = sb("scatter_i", [P, NS], I32)
        slot_past = sb("slot_past", [P, NS, E])
        count_past = sb("count_past", [P, NS, E - 1])
        tokens_past = sb("tokens_past", [P, NS])
        slot_exp = sb("slot_exp", [P, NS])
        slot_exp_i = sb("slot_exp_i", [P, NS], I32)
        sh_silu = sb("sh_silu", [P, 2, L])
        sh_hid = sb("sh_hid", [P, 4, L])
        zg = sb("zg", [P, RING, ZW])
        xsT = sb("xsT", [P, 2, P])
        xs_hi = sb("xs_hi", [P, 2, P], F32R)
        xs_lo = sb("xs_lo", [P, 2, P], F32R)
        sl_hidT = sb("sl_hidT", [P, 2, IC, P])
        y_sl = w_gu_sb[:, 0:NS * H].rearrange("p (s h) -> p s h", s=NS)
        sl_silu = w_gu_sb[:, NS * H:NS * H + 2 * I].rearrange("p (k i) -> p k i", k=2)
        sl_hid = w_gu_sb[:, NS * H + 2 * I:NS * H + 4 * I].rearrange("p (k i) -> p k i", k=2)

        S = [bank("S0"), bank("S1")]
        PT = [bank("PT0"), bank("PT1")]
        O = [bank("O0"), bank("O1")]
        M = [bank("M0"), bank("M1")]

        ld_x = [sem(f"ld_x{b}") for b in range(B)]
        ld_vec, ld_bv, ld_wmod, ld_wqkv = sem("ld_vec"), sem("ld_bv"), sem("ld_wmod"), sem("ld_wqkv")
        ld_router, ld_sh_gu, ld_sh_down = sem("ld_router"), sem("ld_sh_gu"), sem("ld_sh_down")
        ld_gu, ld_down = sem("ld_gu"), sem("ld_down")
        c_set = sem("c_set")
        c_done = sem("c_done")
        vec_up, cols_done, silu_done = sem("vec_up"), sem("cols_done"), sem("silu_done")
        modc_up, modc_done = sem("modc_up"), sem("modc_done")
        modr_up, modr_raw, modr_done = sem("modr_up"), sem("modr_raw"), sem("modr_done")
        row_up, bc_done, ga_up, wv_done = sem("row_up"), sem("bc_done"), sem("ga_up"), sem("wv_done")
        shd_done, gate_copied = sem("shd_done"), sem("gate_copied")
        st1_done, mv1_done, r1_done, norm_done = sem("st1_done"), sem("mv1_done"), sem("r1_done"), sem("norm_done")
        nT_up, hT_done = sem("nT_up"), sem("hT_done")
        q_up, qT_done, k_up, kT_done, v_up, v_done = (sem(n) for n in ("q_up", "qT_done", "k_up", "kT_done", "v_up", "v_done"))
        s_up, max_done, p_done = sem("s_up"), sem("max_done"), sem("p_done")
        pT_up, pT_done, o_up, x1_done = sem("pT_up"), sem("pT_done"), sem("o_up"), sem("x1_done")
        xres_done, inv_done = sem("xres_done"), sem("inv_done")
        st2_done, mv2_done, h2u_done, h2_done = sem("st2_done"), sem("mv2_done"), sem("h2u_done"), sem("h2_done")
        st3_done, mv3_done, z_done, w_done = sem("st3_done"), sem("mv3_done"), sem("z_done"), sem("w_done")
        gh2_done, xb_done = sem("gh2_done"), sem("xb_done")
        zT_up, xfT_done, xf_split, lg_up, lg_done = sem("zT_up"), sem("xfT_done"), sem("xf_split"), sem("lg_up"), sem("lg_done")
        xf_hi_done, w_hi_done, w_lo_done, sh_hi_done, sh_lo_done = (sem(n) for n in ("xf_hi_done", "w_hi_done", "w_lo_done", "sh_hi_done", "sh_lo_done"))
        top_done, tanh_done, hot_done, seen_done = sem("top_done"), sem("tanh_done"), sem("hot_done"), sem("seen_done")
        rank_up, rank_read, rmod_done, rowhot_done = sem("rank_up"), sem("rank_read"), sem("rmod_done"), sem("rowhot_done")
        z_stored = sem("z_stored")
        cnt_read, sval_done, table_up, table_read = sem("cnt_read"), sem("sval_done"), sem("table_up"), sem("table_read")
        gidx_done, sidx_done, sexp_done = sem("gidx_done"), sem("sidx_done"), sem("sexp_done")
        shg_up, shu_up, shsilu_done, shhid_done = sem("shg_up"), sem("shu_up"), sem("shsilu_done"), sem("shhid_done")
        shd_up, base_done, base_stored = sem("shd_up"), sem("base_done"), sem("base_stored")
        gathered = [sem(f"gathered{s}") for s in range(NS)]
        xs_up, xs_done, xhi_done, xlo_done = sem("xs_up"), sem("xs_done"), sem("xhi_done"), sem("xlo_done")
        gu_up, ss_done, sh_done = sem("gu_up"), sem("ss_done"), sem("sh_done")
        ht_up, ht_done, y_up, y_done = sem("ht_up"), sem("ht_done"), sem("y_up"), sem("y_done")
        scattered = sem("scattered")
        dve_step = sem("dve_step")

        x_v = x.rearrange("(b p t) h -> b p t h", p=P, t=T)
        out_v = out[0:B * L, :].rearrange("(b p t) h -> b p t h", p=P, t=T)
        z_v = z_rows.rearrange("(b p t) w -> b p t w", p=P, t=T)
        CONSTS = 17
        WC = E * 2 * I // B
        SH_BANKS = [M, S, PT, S, PT, S, PT, S]

        def tiles(buf, b):
            return buf[:, T * b:T * b + T]

        def over(ap, shape):
            return ap.broadcast_to(shape)

        block = ctx.enter_context(nc.Block())

        @block.sync
        def _(sp):
            sp.dma_start(vec_rows[:, :], vecs).then_inc(ld_vec, 16)
            sp.dma_start(tiles(xs, 0), x_v[0]).then_inc(ld_x[0], 16)
            sp.dma_start(wmod_sb[:, :], wmod).then_inc(ld_wmod, 16)
            sp.dma_start(wqkv_sb[:, :, :], wqkv).then_inc(ld_wqkv, 16)
            sp.dma_start(bv_rows[:, :], bv.partition_broadcast(B)).then_inc(ld_bv, 16)
            for b in range(1, B):
                sp.dma_start(tiles(xs, b), x_v[b]).then_inc(ld_x[b], 16)
            sp.dma_start(router_sb[:, :], router_w).then_inc(ld_router, 16)
            sp.dma_start(sh_gu_sb[:, :], sh_gu).then_inc(ld_sh_gu, 16)
            sp.dma_start(sh_down_sb[:, :, :], sh_down).then_inc(ld_sh_down, 16)
            sp.dma_start(w_gu_sb[:, :], w_gu).then_inc(ld_gu, 16)
            sp.dma_start(w_down_sb[:, :], w_down).then_inc(ld_down, 16)
            sp.wait_ge(ld_down, 16)
            sp.dma_start(out[B * L:, :].rearrange("(p j) h -> p (j h)", p=P), w_down_sb[:, 0:NPAD // P * H]).then_inc(base_stored, 16)
            sp.wait_ge(z_done, NT)
            sp.wait_ge(gate_copied, B)
            sp.wait_ge(w_done, 1)
            for b in range(B):
                sp.dma_start(z_v[b], tiles(zw, b)).then_inc(z_stored, 16)
            for b in range(B):
                sp.wait_ge(base_done, b + 1)
                sp.dma_start(out_v[b], tiles(xs, b)).then_inc(base_stored, 16)
            sp.wait_ge(base_stored, 16 * (B + 1))
            sp.wait_ge(z_stored, 16 * B)
            sp.wait_ge(scattered, 16 * NS)

        @block.gpsimd
        def _(pool):
            def hot(buf, fill):
                pool.affine_select(out=buf[:, :], in_=buf[:, :], pattern=[[-1, P]], base=0, channel_multiplier=1,
                                   compare_op=ALU.not_equal, fill=fill).then_inc(c_done, 1)

            def ramp(buf, pattern, base=0, channel=0):
                pool.iota(buf, pattern=pattern, base=base, channel_multiplier=channel,
                          allow_small_or_imprecise_dtypes=True).then_inc(c_done, 1)

            pool.memset(ident[:, :], 0.0).then_inc(c_set, 1)
            pool.memset(pick_b[:, :, :], 0.0).then_inc(c_set, 1)
            pool.memset(mask_diag[:, :], 0.0).then_inc(c_set, 1)
            pool.memset(ident_b[:, :], 0.0).then_inc(c_set, 1)
            pool.memset(not_before[:, :], -1.0).then_inc(c_set, 1)
            pool.memset(earlier_e[:, :, :], 1.0).then_inc(c_set, 1)
            pool.memset(same_e[:, :, :], 1.0).then_inc(c_set, 1)
            pool.wait_ge(c_set, 1)
            hot(ident, 1.0)
            pool.wait_ge(c_set, 7)
            pool.affine_select(out=pick_b[:, :, :], in_=pick_b[:, :, :], pattern=[[-1, B], [0, P]], base=0,
                               channel_multiplier=1, compare_op=ALU.not_equal, fill=1.0).then_inc(c_done, 1)
            hot(mask_diag, LOWEST)
            hot(ident_b, 1.0)
            pool.memset(ones_b[:, :], 1.0).then_inc(c_done, 1)
            ramp(steps_128[:, :], [[P, NT]])
            ramp(iota_p[:, :], [[1, P]])
            ramp(iota_e[:, :], [[1, E]])
            ramp(iota_e8[:, :], [[1, E]], base=-E)
            ramp(iota_s[:, :], [[1, NS]])
            ramp(pad_base[:, :], [[P, NS]], base=B * L + 8, channel=1)
            ramp(batch_512[:, :], [[L, B], [0, T]])
            ramp(tile_8[:, :], [[0, B], [1, T]], base=8)
            ramp(part_4[:, :], [[0, 1]], channel=T)
            pool.affine_select(out=not_before[:, :], in_=not_before[:, :], pattern=[[-1, P]], base=0, channel_multiplier=1,
                               compare_op=ALU.is_ge, fill=0.0).then_inc(c_done, 1)
            pool.affine_select(out=earlier_e[:, :, :], in_=earlier_e[:, :, :], pattern=[[1, E], [-1, E]], base=0,
                               channel_multiplier=0, compare_op=ALU.is_gt, fill=0.0).then_inc(c_done, 1)
            pool.affine_select(out=same_e[:, :, :], in_=same_e[:, :, :], pattern=[[0, E], [1, NT]], base=0,
                               channel_multiplier=0, compare_op=ALU.is_gt, fill=0.0).then_inc(c_done, 1)

            def residual(b):
                pool.wait_ge(norm_done, T * (b + 1))
                pool.wait_ge(bc_done, b + 1)
                pool.tensor_tensor(tiles(xs, b), tiles(xs, b), over(bc[:, b, 3:4, :], [P, T, H]),
                                   ALU.add).then_inc(xres_done, 1)

            def gates(b):
                pool.wait_ge(bc_done, b + 1)
                pool.tensor_tensor(sh_down_gb[:, b], sh_down_sb[:, :, :], over(bc[:, b, 0:1, :], [P, IC, H]),
                                   ALU.mult).then_inc(shd_done, 1)
                pool.tensor_copy(tiles(zw, b)[:, :, H + 1:], over(bc[:, b, 0:1, :], [P, T, H])).then_inc(gate_copied, 1)

            def base_rows(b):
                pool.wait_ge(h2_done, T * (b + 1))
                if b >= 1:
                    pool.wait_ge(xb_done, b)
                pool.tensor_tensor(gh2[:, :, :], h2[:, :, :], over(bc[:, b, 0:1, :], [P, T, H]), ALU.mult).then_inc(gh2_done, 1)
                pool.wait_ge(gh2_done, b + 1)
                pool.tensor_tensor(tiles(xs, b), gh2[:, :, :], tiles(xs, b), ALU.add).then_inc(xb_done, 1)

            def split_rows(b):
                pool.wait_ge(xf_hi_done, b + 1)
                pool.tensor_tensor(xf_lo[:, b, :], xfT[:, :], xf_hi[:, b, :].bitcast(F32), ALU.subtract).then_inc(xf_split, 1)

            def split_weights(b):
                c = slice(WC * b, WC * (b + 1))
                pool.wait_ge(w_hi_done, b + 1)
                pool.tensor_tensor(w_gu_lo[:, c], w_gu_sb[:, c], w_gu_hi[:, c].bitcast(F32), ALU.subtract).then_inc(w_lo_done, 1)

            residual(0)
            pool.wait_ge(ld_sh_down, 16)
            gates(0)
            for b in range(B):
                if b + 1 < B:
                    residual(b + 1)
                    gates(b + 1)
                if b == 1:
                    pool.wait_ge(sh_hi_done, 1)
                    pool.tensor_tensor(sh_gu_lo[:, :], sh_gu_sb[:, :], sh_gu_hi[:, :].bitcast(F32), ALU.subtract).then_inc(sh_lo_done, 1)
                if b >= 1:
                    base_rows(b - 1)
                    split_rows(b - 1)
                split_weights(b)
            base_rows(B - 1)
            split_rows(B - 1)

            def gather(s):
                if s >= RING:
                    pool.wait_ge(y_done, s - RING + 1)
                pool.indirect_dma_start(out=zg[:, s % RING, :], out_offset=None, in_=z_rows,
                                        in_offset=bass.IndirectOffsetOnAxis(ap=gather_i[:, s:s + 1], axis=0)
                                        ).then_inc(gathered[s], 16)

            pool.wait_ge(gidx_done, 1)
            pool.wait_ge(z_stored, 16 * B)
            for s in range(RING):
                gather(s)
            pool.wait_ge(sidx_done, 1)
            pool.wait_ge(base_stored, 16 * (B + 1))
            for s in range(NS):
                if s + RING < NS:
                    gather(s + RING)
                pool.wait_ge(y_done, s + 1)
                pool.indirect_dma_start(out=out, out_offset=bass.IndirectOffsetOnAxis(ap=scatter_i[:, s:s + 1], axis=0),
                                        in_=y_sl[:, s, :], in_offset=None, compute_op=ALU.add).then_inc(scattered, 16)

        @block.scalar
        def _(act):
            def norm1(b):
                act.wait_ge(r1_done, 1 if b == 0 else 2)
                if b >= 1:
                    act.wait_ge(nT_up, b)
                for t in range(T):
                    n = T * b + t
                    act.activation(normed[:, t, :], xs[:, n, :], ACT.Identity, bias=nmr1[:, n:n + 1],
                                   scale=r1[:, n:n + 1]).then_inc(norm_done, 1)

            def h_rows(b):
                act.wait_ge(nT_up, b + 1)
                act.activation(hT[:, :], M[0][:, :], ACT.Identity, bias=shift_a[:, b:b + 1],
                               scale=scale_a[:, b:b + 1]).then_inc(hT_done, 1)

            def q_rows(b):
                act.wait_ge(q_up, b + 1)
                act.activation(qT[:, :], M[1][:, :], ACT.Identity, bias=bq_h[:, 0:1], scale=1.0 / H).then_inc(qT_done, 1)

            def k_rows(b):
                act.wait_ge(k_up, b + 1)
                act.activation(kT[:, :], M[0][:, :], ACT.Identity, bias=cols[:, 1:2]).then_inc(kT_done, 1)

            def v_rows(b):
                act.wait_ge(v_up, b + 1)
                act.activation(v_sb[:, b % 2], M[1][:, :].rearrange("p (t h) -> p t h", t=T), ACT.Copy).then_inc(v_done, 1)

            def exps(n):
                act.wait_ge(max_done, n + 1)
                if n >= 2:
                    act.wait_ge(pT_up, n - 1)
                act.activation(probs[:, n % 2, :], S[n % 2][:, :], ACT.Exp, bias=neg_max[:, n:n + 1],
                               accum_out=prob_sum[:, n:n + 1]).then_inc(p_done, 1)

            def probs_T(n):
                act.wait_ge(pT_up, n + 1)
                if n >= 2:
                    act.wait_ge(o_up, n - 1)
                act.activation(probsT[:, n % 2, :], PT[n % 2][:, :], ACT.Copy).then_inc(pT_done, 1)

            def xf_rows(b):
                act.wait_ge(zT_up, b + 1)
                if b >= 1:
                    act.wait_ge(lg_up, b)
                    act.wait_ge(xf_split, b)
                act.activation(xfT[:, :], M[0][:, :], ACT.Identity, bias=cols[:, 3:4], scale=cols[:, 2:3]).then_inc(xfT_done, 1)
                act.wait_ge(xfT_done, b + 1)
                act.activation(xf_hi[:, b, :], xfT[:, :], ACT.Copy).then_inc(xf_hi_done, 1)

            def weights_hi(b):
                c = slice(WC * b, WC * (b + 1))
                act.activation(w_gu_hi[:, c], w_gu_sb[:, c], ACT.Copy).then_inc(w_hi_done, 1)

            def shared_silu(k):
                act.wait_ge(shg_up, k + 1)
                if k >= 2:
                    act.wait_ge(shhid_done, k - 1)
                act.activation(sh_silu[:, k % 2, :], SH_BANKS[k][0][:, :], ACT.Silu).then_inc(shsilu_done, 1)

            def score_tanh():
                act.wait_ge(top_done, 1)
                act.activation(tanh_top[:, :], top[:, :], ACT.Tanh, scale=0.5).then_inc(tanh_done, 1)

            act.wait_ge(cols_done, 1)
            act.activation(silu_c[:, :], cols[:, 4:8], ACT.Silu).then_inc(silu_done, 1)
            act.wait_ge(cols_done, 2)
            norm1(0)
            act.wait_ge(modc_done, 2)
            h_rows(0)
            q_rows(0)
            k_rows(0)
            for b in range(B):
                act.wait_ge(row_up, b + 1)
                bank = (PT[1], O[1], S[0], S[1])[b]
                act.activation(bc[:, b, :, :], bank[:, :].rearrange("p (j h) -> p j h", j=4), ACT.Copy).then_inc(bc_done, 1)
            v_rows(0)
            norm1(1)
            exps(0)
            exps(1)
            for b in range(B):
                n = T * b
                nxt = b + 1 < B
                probs_T(n)
                if nxt and b >= 1:
                    norm1(b + 1)
                exps(n + 2)
                probs_T(n + 1)
                if nxt:
                    h_rows(b + 1)
                exps(n + 3)
                probs_T(n + 2)
                if nxt:
                    q_rows(b + 1)
                    k_rows(b + 1)
                else:
                    shared_silu(0)
                probs_T(n + 3)
                if nxt:
                    v_rows(b + 1)
                else:
                    shared_silu(1)
                if b == 0:
                    act.wait_ge(ld_sh_gu, 16)
                    act.activation(sh_gu_hi[:, :], sh_gu_sb[:, :], ACT.Copy).then_inc(sh_hi_done, 1)
                    act.wait_ge(ld_gu, 16)
                if b >= 1:
                    xf_rows(b - 1)
                if nxt:
                    exps(n + T)
                weights_hi(b)
                if nxt:
                    exps(n + T + 1)
            shared_silu(2)
            shared_silu(3)
            xf_rows(B - 1)
            score_tanh()
            for k in range(4, 2 * B):
                shared_silu(k)
            act.wait_ge(w_lo_done, B)
            for s in range(NS + 2):
                if s < NS:
                    act.wait_ge(xs_up, s + 1)
                    if s >= 2:
                        act.wait_ge(xlo_done, s - 1)
                    act.activation(xsT[:, s % 2, :], M[s % 2][:, 0:P], ACT.Identity, bias=cols[:, 3:4],
                                   scale=cols[:, 2:3]).then_inc(xs_done, 1)
                if 1 <= s <= NS:
                    k = s - 1
                    act.wait_ge(gu_up, k + 1)
                    if k >= 2:
                        act.wait_ge(sh_done, k - 1)
                    act.activation(sl_silu[:, k % 2, :], S[k % 2][:, 0:I], ACT.Silu,
                                   scale=zg[:, k % RING, H:H + 1]).then_inc(ss_done, 1)
                if s >= 2:
                    k = s - 2
                    act.wait_ge(ht_up, k + 1)
                    if k >= 2:
                        act.wait_ge(y_up, k - 1)
                    act.activation(sl_hidT[:, k % 2], PT[k % 2][:, 0:I].rearrange("p (c q) -> p c q", c=IC),
                                   ACT.Copy).then_inc(ht_done, 1)

        @block.vector
        def _(dve):
            small = Steps(dve, dve_step)

            def rsqrt(v, t, r, mv, lo, hi, done=None, between=()):
                v, t, r = v[:, lo:hi], t[:, lo:hi], r[:, lo:hi]
                between = list(between)

                def other():
                    if between:
                        between.pop(0)()

                small.then(dve.tensor_scalar(v, mv[:, lo:hi, 1], EPS, None, ALU.add))
                other()
                small.done()
                small.then(dve.tensor_scalar(r.bitcast(I32), v.bitcast(I32), -0.5, RSQRT_MAGIC, ALU.mult, ALU.add))
                for step in range(3):
                    other()
                    small.done()
                    small.then(dve.tensor_tensor(t, r, r, ALU.mult))
                    other()
                    small.done()
                    small.then(dve.scalar_tensor_tensor(out=t, in0=t, scalar=-0.5, in1=v, op0=ALU.mult, op1=ALU.mult))
                    other()
                    small.done()
                    small.then(dve.scalar_tensor_tensor(out=r, in0=t, scalar=1.5, in1=r, op0=ALU.add, op1=ALU.mult))
                while between:
                    other()
                small.done()

            def norm1_stats(lo, hi, k, between=()):
                for n in range(lo, hi):
                    dve.bn_stats(st1[:, n, :], xs[:, n, :]).then_inc(st1_done, 1)
                for n in range(lo, hi):
                    dve.wait_ge(st1_done, n + 1)
                    dve.bn_aggr(mv1[:, n, :], st1[:, n, :]).then_inc(mv1_done, 1)
                dve.wait_ge(mv1_done, hi)
                rsqrt(v1, t1, r1, mv1, lo, hi, between=between)
                dve.scalar_tensor_tensor(out=nmr1[:, lo:hi], in0=mv1[:, lo:hi, 0], scalar=-1.0, in1=r1[:, lo:hi],
                                         op0=ALU.mult, op1=ALU.mult).then_inc(r1_done, 1)

            def score_max(n):
                dve.wait_ge(s_up, n + 1)
                dve.tensor_reduce(neg_max[:, n:n + 1], S[n % 2][:, :], AX_X, ALU.max, negate=True).then_inc(max_done, 1)

            def invert_sum(n):
                dve.wait_ge(p_done, n + 1)
                dve.reciprocal(prob_inv[:, n:n + 1], prob_sum[:, n:n + 1]).then_inc(inv_done, 1)

            def attention_out(n):
                dve.wait_ge(inv_done, n + 1)
                dve.wait_ge(xres_done, n // T + 1)
                dve.wait_ge(o_up, n + 1)
                dve.scalar_tensor_tensor(out=xs[:, n, :], in0=O[n % 2][:, 0:H], scalar=prob_inv[:, n:n + 1],
                                         in1=xs[:, n, :], op0=ALU.mult, op1=ALU.add).then_inc(x1_done, 1)

            def norm2_stats(b):
                for n in range(T * b, T * b + T):
                    dve.wait_ge(x1_done, n + 1)
                    dve.bn_stats(st2[:, n, :], xs[:, n, :]).then_inc(st2_done, 1)
                for n in range(T * b, T * b + T):
                    dve.wait_ge(st2_done, n + 1)
                    dve.bn_aggr(mv2[:, n, :], st2[:, n, :]).then_inc(mv2_done, 1)
                dve.wait_ge(mv2_done, T * (b + 1))

            def norm2_centre(n):
                b, t = n // T, n % T
                dve.scalar_tensor_tensor(out=h2u[:, t, :], in0=xs[:, n, :], scalar=mv2[:, n, 0:1], in1=bc[:, b, 2, :],
                                         op0=ALU.subtract, op1=ALU.mult).then_inc(h2u_done, 1)

            def norm2(b, between=()):
                lo, hi = T * b, T * b + T
                norm2_stats(b)
                if b >= 1:
                    dve.wait_ge(h2_done, lo)
                rsqrt(v2, t2, r2, mv2, lo, hi,
                      between=[lambda n=n: norm2_centre(n) for n in range(lo, hi)] + list(between))
                if b >= 1:
                    dve.wait_ge(gh2_done, b)
                for n in range(lo, hi):
                    dve.wait_ge(h2u_done, n + 1)
                    dve.scalar_tensor_tensor(out=h2[:, n - lo, :], in0=h2u[:, n - lo, :], scalar=r2[:, n:n + 1], in1=bc[:, b, 1, :],
                                             op0=ALU.mult, op1=ALU.add).then_inc(h2_done, 1)

            def norm3(b, between=()):
                lo, hi = T * b, T * b + T
                for n in range(lo, hi):
                    dve.wait_ge(h2_done, n + 1)
                    dve.bn_stats(st3[:, n, :], h2[:, n - lo, :]).then_inc(st3_done, 1)
                for n in range(lo, hi):
                    dve.wait_ge(st3_done, n + 1)
                    dve.bn_aggr(mv3[:, n, :], st3[:, n, :]).then_inc(mv3_done, 1)
                dve.wait_ge(mv3_done, hi)
                rsqrt(v3, t3, r3, mv3, lo, hi, between=between)
                for n in range(lo, hi):
                    dve.tensor_scalar(zw[:, n, 0:H], h2[:, n - lo, :], mv3[:, n, 0:1], r3[:, n:n + 1],
                                      ALU.subtract, ALU.mult).then_inc(z_done, 1)

            def logits_out(b):
                dve.wait_ge(lg_up, b + 1)
                dve.tensor_copy(tiles(lg, b), M[1][:, 0:T * E].rearrange("p (t e) -> p t e", t=T)).then_inc(lg_done, 1)

            def shared_hidden(k):
                dve.wait_ge(shsilu_done, k + 1)
                dve.wait_ge(shu_up, k + 1)
                if k >= 4:
                    dve.wait_ge(shd_up, (k - 4) // IC + 1)
                dve.tensor_tensor(sh_hid[:, k % 4, :], sh_silu[:, k % 2, :], SH_BANKS[k][1][:, :], ALU.mult).then_inc(shhid_done, 1)

            def shared_out(b):
                dve.wait_ge(shd_up, b + 1)
                dve.wait_ge(xb_done, b + 1)
                dve.tensor_tensor(tiles(xs, b), O[b % 2][:, :].rearrange("p (t h) -> p t h", t=T), tiles(xs, b),
                                  ALU.add).then_inc(base_done, 1)

            def route():
                dve.wait_ge(lg_done, B)
                dve.tensor_reduce(top[:, :], lg[:, :, :], AX_X, ALU.max).then_inc(top_done, 1)
                dve.wait_ge(top_done, 1)
                small.chain(dve.tensor_tensor(is_top[:, :, :], lg[:, :, :], over(top[:, :].unsqueeze(2), [P, NT, E]), ALU.is_equal))
                small.chain(dve.scalar_tensor_tensor(out=cand[:, :, :], in0=is_top[:, :, :], scalar=-float(E),
                                                     in1=over(iota_e[:, :].unsqueeze(1), [P, NT, E]), op0=ALU.mult, op1=ALU.add))
                small.chain(dve.tensor_reduce(first[:, :], cand[:, :, :], AX_X, ALU.min))
                dve.tensor_tensor(onehot[:, :, :], over(iota_e8[:, :].unsqueeze(2), [P, E, NT]),
                                  over(first[:, :].unsqueeze(1), [P, E, NT]), ALU.is_equal).then_inc(hot_done, 1)
                dve.wait_ge(hot_done, 1)
                dve.tensor_tensor_scan(seen[:, :, :].rearrange("p e n -> p (e n)"), same_e[:, :, :].rearrange("p e n -> p (e n)"),
                                       onehot[:, :, :].rearrange("p e n -> p (e n)"), 0.0, ALU.mult, ALU.add).then_inc(seen_done, 1)
                dve.wait_ge(tanh_done, 1)
                dve.tensor_scalar(zw[:, :, H], tanh_top[:, :], 0.5, 0.5, ALU.mult, ALU.add).then_inc(w_done, 1)

            def slot_tables():
                onehot_ne = onehot[:, :, :].rearrange("p e n -> p n e")
                dve.wait_ge(rank_up, 1)
                dve.tensor_tensor(rank_of[:, :, :], M[1][:, 128:256].rearrange("p (e n) -> p n e", e=E), onehot_ne,
                                  ALU.mult).then_inc(rank_read, 1)
                dve.tensor_copy(count[:, :], M[1][:, 256:256 + E]).then_inc(cnt_read, 1)
                dve.wait_ge(rank_read, 1)
                small.then(dve.tensor_reduce(rank[:, :], rank_of[:, :, :], AX_X, ALU.add))
                dve.wait_ge(cnt_read, 1)
                small.chain(dve.tensor_tensor(count_over[:, :, :], over(count[:, :].unsqueeze(2), [P, E, NT]),
                                              over(steps_128[:, :].unsqueeze(1), [P, E, NT]), ALU.is_gt))
                small.then(dve.tensor_scalar(rank_128[:, :], rank[:, :], -(P - 1) / 2, 1.0 / P, ALU.add, ALU.mult))
                small.chain(dve.tensor_reduce(slots_of[:, :], count_over[:, :, :], AX_X, ALU.add))
                small.then(dve.tensor_scalar(rank_div[:, :], rank_128[:, :], ROUND, -ROUND, ALU.add, ALU.add))
                small.chain(dve.tensor_tensor(slots_before[:, :, :], over(slots_of[:, :].unsqueeze(1), [P, E, E]),
                                              earlier_e[:, :, :], ALU.mult))
                dve.scalar_tensor_tensor(out=rank_mod[:, :], in0=rank_div[:, :], scalar=-float(P), in1=rank[:, :],
                                         op0=ALU.mult, op1=ALU.add).then_inc(rmod_done, 1)
                small.chain(dve.tensor_reduce(slot0[:, :], slots_before[:, :, :], AX_X, ALU.add))
                row_hots(0)
                small.chain(dve.tensor_tensor(slot_pick[:, :, :], onehot_ne, over(slot0[:, :].unsqueeze(1), [P, NT, E]), ALU.mult))
                row_hots(1)
                small.chain(dve.tensor_reduce(slot_first[:, :], slot_pick[:, :, :], AX_X, ALU.add))
                row_hots(2)
                small.chain(dve.tensor_tensor(slot[:, :], slot_first[:, :], rank_div[:, :], ALU.add))
                row_hots(3)
                small.chain(dve.tensor_tensor(slot_diff[:, :, :], over(slot[:, :].unsqueeze(2), [P, NT, NS]),
                                              over(iota_s[:, :].unsqueeze(1), [P, NT, NS]), ALU.subtract))
                for j, part in enumerate((tile_8, batch_512)):
                    dve.scalar_tensor_tensor(out=slot_val[:, :, j, :], in0=slot_diff[:, :, :], scalar=0.0,
                                             in1=over(part[:, :].unsqueeze(2), [P, NT, NS]), op0=ALU.is_equal,
                                             op1=ALU.mult).then_inc(sval_done, 1)
                dve.tensor_scalar(slot_val[:, :, 2, :], slot_diff[:, :, :], 0.0, part_4[:, 0:1], ALU.is_equal,
                                  ALU.mult).then_inc(sval_done, 1)

            def row_hots(b):
                if b == 0:
                    dve.wait_ge(rmod_done, 1)
                for n in range(T * b, T * b + T):
                    dve.tensor_scalar(row_hot[:, n, :], iota_p[:, :], rank_mod[:, n:n + 1], None, ALU.is_equal).then_inc(rowhot_done, 1)

            def slot_experts():
                small.chain(dve.tensor_tensor(slot_end[:, :], slot0[:, :], slots_of[:, :], ALU.add))
                small.chain(dve.tensor_tensor(slot_past[:, :, :], over(slot_end[:, :].unsqueeze(1), [P, NS, E]),
                                              over(iota_s[:, :].unsqueeze(2), [P, NS, E]), ALU.is_le))
                small.then(dve.tensor_reduce(slot_exp[:, :], slot_past[:, :, :], AX_X, ALU.add))
                small.chain(dve.tensor_tensor(count_past[:, :, :], slot_past[:, :, 0:E - 1], over(count[:, 1:E].unsqueeze(1), [P, NS, E - 1]),
                                              ALU.mult))
                dve.tensor_scalar(slot_exp_i[:, :], slot_exp[:, :], float(E - 1), None, ALU.min).then_inc(sexp_done, 1)
                small.chain(dve.tensor_reduce(tokens_past[:, :], count_past[:, :, :], AX_X, ALU.add))
                small.chain(dve.scalar_tensor_tensor(out=pad_row[:, :], in0=tokens_past[:, :], scalar=count[:, 0:1], in1=pad_base[:, :],
                                                     op0=ALU.add, op1=ALU.subtract))

            def token_tables():
                dve.wait_ge(table_up, 1)
                dve.tensor_copy(table[:, :, :], M[0][:, 0:3 * NS].rearrange("p (j s) -> p j s", j=3)).then_inc(table_read, 1)
                dve.wait_ge(table_read, 1)
                small.chain(dve.scalar_tensor_tensor(out=token_ab[:, :], in0=table[:, 0, :], scalar=-8.0, in1=table[:, 1, :],
                                                     op0=ALU.add, op1=ALU.add))
                small.chain(dve.tensor_tensor(token[:, :], token_ab[:, :], table[:, 2, :], ALU.add))
                dve.tensor_scalar(gather_i[:, :], token[:, :], 0.0, None, ALU.max).then_inc(gidx_done, 1)
                small.chain(dve.scalar_tensor_tensor(out=pad_or_0[:, :], in0=table[:, 0, :], scalar=8.0, in1=pad_row[:, :],
                                                     op0=ALU.is_lt, op1=ALU.mult))
                dve.tensor_tensor(scatter_i[:, :], token[:, :], pad_or_0[:, :], ALU.subtract).then_inc(sidx_done, 1)

            dve.wait_ge(vec_up, 1)
            dve.tensor_copy(cols[:, :], M[0][:, 0:8]).then_inc(cols_done, 1)
            dve.wait_ge(cols_done, 1)
            dve.tensor_scalar(bq_h[:, :], cols[:, 0:1], 1.0 / H, None, ALU.mult).then_inc(cols_done, 1)
            dve.wait_ge(ld_x[0], 16)
            norm1_stats(0, T, 0)
            dve.wait_ge(modc_up, 1)
            dve.tensor_copy(shift_a[:, :], M[1][:, 0:B]).then_inc(modc_done, 1)
            dve.tensor_scalar(scale_a[:, :], M[1][:, B:2 * B], 1.0, None, ALU.add).then_inc(modc_done, 1)
            dve.wait_ge(modr_up, 1)
            dve.tensor_copy(mod_raw[:, :, :], PT[0][0:B, :].rearrange("p (j h) -> p j h", j=4)).then_inc(modr_raw, 1)
            dve.wait_ge(modr_raw, 1)
            gates = mod_raw[:, 0:4:3, :]
            small.then(dve.tensor_scalar(gate_sign[:, :, :], gates, 0.0, -0.5, ALU.is_ge, ALU.add))
            small.chain(dve.scalar_tensor_tensor(out=gate_abs[:, :, :], in0=gates, scalar=-1.0, in1=gates, op0=ALU.mult, op1=ALU.max))
            small.chain(dve.scalar_tensor_tensor(out=gate_half[:, :, :], in0=gate_abs[:, :, :], scalar=0.25, in1=gate_sign[:, :, :],
                                                 op0=ALU.max, op1=ALU.mult))
            dve.tensor_scalar(mod_rows[:, 0:2, :], gate_half[:, :, :], 2.0, None, ALU.mult).then_inc(modr_done, 1)
            dve.tensor_copy(mod_rows[:, 2, :], mod_raw[:, 1, :]).then_inc(modr_done, 1)
            dve.tensor_scalar(mod_rows[:, 3, :], mod_raw[:, 2, :], 1.0, None, ALU.add).then_inc(modr_done, 1)
            dve.wait_ge(ld_bv, 16)
            dve.wait_ge(modr_done, 1)
            dve.tensor_tensor(mod_rows[:, 4, :], mod_rows[:, 0, :], bv_rows[:, :], ALU.mult).then_inc(modr_done, 1)
            for b in range(1, B):
                dve.wait_ge(ld_x[b], 16)
            norm1_stats(T, NT, 1)
            dve.wait_ge(ld_wqkv, 16)
            dve.wait_ge(ga_up, 1)
            dve.tensor_tensor(wv_ga[:, :, :], over(wqkv_sb[:, 2:3, :], [P, B, H]), O[0][:, :].rearrange("p (b h) -> p b h", b=B),
                              ALU.mult).then_inc(wv_done, 1)
            score_max(0)
            score_max(1)
            invert_sum(0)
            dve.wait_ge(c_done, CONSTS)
            for b in range(B):
                n = T * b
                nxt = b + 1 < B
                if b >= 1:
                    norm2(b - 1, between=[lambda: score_max(n + 2), lambda: invert_sum(n + 1), lambda: attention_out(n)])
                else:
                    score_max(n + 2)
                    invert_sum(n + 1)
                    attention_out(n)
                score_max(n + 3)
                invert_sum(n + 2)
                attention_out(n + 1)
                if b >= 1:
                    norm3(b - 1, between=[lambda: attention_out(n + 2), lambda: invert_sum(n + 3)])
                else:
                    attention_out(n + 2)
                    invert_sum(n + 3)
                if not nxt:
                    shared_hidden(0)
                attention_out(n + 3)
                if nxt:
                    score_max(n + T)
                    score_max(n + T + 1)
                    invert_sum(n + T)
                if b >= 1:
                    logits_out(b - 1)
            norm2(B - 1, between=[lambda: shared_hidden(1)])
            norm3(B - 1, between=[lambda: shared_hidden(2), lambda: shared_hidden(3)])
            shared_out(0)
            logits_out(B - 1)
            route()
            slot_tables()
            shared_hidden(4)
            slot_experts()
            shared_hidden(5)
            shared_out(1)
            token_tables()
            shared_hidden(6)
            shared_hidden(7)
            shared_out(2)
            shared_out(3)
            for s in range(NS + 3):
                if s < NS:
                    if s >= 2:
                        dve.wait_ge(gu_up, s - 1)
                    dve.wait_ge(xs_done, s + 1)
                    dve.tensor_copy(xs_hi[:, s % 2, :], xsT[:, s % 2, :]).then_inc(xhi_done, 1)
                    dve.wait_ge(xhi_done, s + 1)
                    dve.tensor_tensor(xs_lo[:, s % 2, :], xsT[:, s % 2, :], xs_hi[:, s % 2, :].bitcast(F32),
                                      ALU.subtract).then_inc(xlo_done, 1)
                if 1 <= s <= NS:
                    k = s - 1
                    dve.wait_ge(ss_done, k + 1)
                    if k >= 2:
                        dve.wait_ge(ht_up, k - 1)
                    dve.scalar_tensor_tensor(out=sl_hid[:, k % 2, :], in0=S[k % 2][:, I:2 * I], scalar=zg[:, k % RING, H:H + 1],
                                             in1=sl_silu[:, k % 2, :], op0=ALU.mult, op1=ALU.mult).then_inc(sh_done, 1)
                if s >= 3:
                    k = s - 3
                    dve.wait_ge(y_up, k + 1)
                    dve.tensor_tensor(y_sl[:, k, :], O[k % 2][:, 0:H], zg[:, k % RING, H + 1:], ALU.mult).then_inc(y_done, 1)

        @block.tensor
        def _(pe):
            def transposes(dst, src_of, count):
                for t in range(count):
                    last = pe.transpose(dst[:, t * P:(t + 1) * P], src_of(t), ident[:, :])
                return last

            def split_product(dst, l_hi, l_lo, r_hi, r_lo):
                pe.matmul(dst, l_hi, r_hi, start=True, stop=False)
                pe.matmul(dst, l_hi, r_lo, start=False, stop=False)
                return pe.matmul(dst, l_lo, r_hi, start=False, stop=True)

            def rows_T(b):
                pe.wait_ge(norm_done, T * (b + 1))
                if b >= 3:
                    pe.wait_ge(xfT_done, b - 2)
                elif b >= 1:
                    pe.wait_ge(kT_done, b)
                else:
                    pe.wait_ge(cols_done, 1)
                transposes(M[0], lambda t: normed[:, t, :], T).then_inc(nT_up, 1)

            def q_product(b):
                pe.wait_ge(hT_done, b + 1)
                if b >= 3:
                    pe.wait_ge(lg_done, b - 2)
                elif b >= 1:
                    pe.wait_ge(v_done, b)
                else:
                    pe.wait_ge(modc_done, 2)
                pe.matmul(M[1][:, :], wqkv_sb[:, 0, :], hT[:, :], start=True, stop=True).then_inc(q_up, 1)

            def k_product(b):
                pe.matmul(M[0][:, :], wqkv_sb[:, 1, :], hT[:, :], start=True, stop=True).then_inc(k_up, 1)

            def v_product(b):
                pe.wait_ge(qT_done, b + 1)
                for t in range(T):
                    last = pe.matmul(M[1][:, t * H:(t + 1) * H], hT[:, t * P:(t + 1) * P], wv_ga[:, b, :], start=True, stop=True)
                last.then_inc(v_up, 1)

            def scores(n):
                b, t = n // T, n % T
                if t == 0:
                    pe.wait_ge(kT_done, b + 1)
                if n >= 2:
                    pe.wait_ge(p_done, n - 1)
                pe.matmul(S[n % 2][:, :], qT[:, t * P:(t + 1) * P], kT[:, :], start=True, stop=False)
                pe.matmul(S[n % 2][:, t * P:(t + 1) * P], ident_b[:, :], mask_diag[:, :], start=False, stop=True).then_inc(s_up, 1)

            def probs_up(n):
                pe.wait_ge(p_done, n + 1)
                if n >= 2:
                    pe.wait_ge(pT_done, n - 1)
                transposes(PT[n % 2], lambda k: probs[:, n % 2, k * P:(k + 1) * P], T).then_inc(pT_up, 1)

            def attend(n):
                pe.wait_ge(pT_done, n + 1)
                if n % T == 0:
                    pe.wait_ge(v_done, n // T + 1)
                if n >= 2:
                    pe.wait_ge(x1_done, n - 1)
                for k in range(T):
                    last = pe.matmul(O[n % 2][:, 0:H], probsT[:, n % 2, k * P:(k + 1) * P], v_sb[:, n // T % 2, k, :], start=(k == 0), stop=(k == T - 1))
                last.then_inc(o_up, 1)

            def z_T(b):
                pe.wait_ge(z_done, T * (b + 1))
                if b + 2 < B:
                    pe.wait_ge(kT_done, b + 3)
                else:
                    pe.wait_ge(xfT_done, b)
                    pe.wait_ge(shsilu_done, 1)
                transposes(M[0], lambda t: zw[:, T * b + t, 0:H], T).then_inc(zT_up, 1)

            def logits(b):
                pe.wait_ge(xfT_done, b + 1)
                if b + 2 < B:
                    pe.wait_ge(v_done, b + 3)
                else:
                    pe.wait_ge(lg_done, b)
                    pe.wait_ge(shhid_done, 1)
                for t in range(T):
                    last = pe.matmul(M[1][:, t * E:(t + 1) * E], xfT[:, t * P:(t + 1) * P], router_sb[:, :], start=True, stop=True)
                last.then_inc(lg_up, 1)

            def rank_product():
                pe.wait_ge(lg_done, B)
                r = M[1][:, 128:256]
                pe.wait_ge(hot_done, 1)
                pe.matmul(r, not_before[:, :], onehot[:, :, :].rearrange("p e n -> p (e n)"), start=True, stop=False)
                pe.wait_ge(seen_done, 1)
                pe.matmul(r, ones_b[:, :], seen[:, :, :].rearrange("p e n -> p (e n)"), start=False, stop=True)
                pe.matmul(M[1][:, 256:256 + E], ones_b[:, :], seen[:, :, NT - 1], start=True, stop=True).then_inc(rank_up, 1)

            def table_product():
                pe.wait_ge(sval_done, 3)
                pe.wait_ge(rowhot_done, NT)
                pe.wait_ge(xfT_done, B)
                for n in range(NT):
                    last = pe.matmul(M[0][:, 0:3 * NS], row_hot[:, n, :], slot_val[:, n, :, :].rearrange("p j s -> p (j s)"),
                                     start=(n == 0), stop=(n == NT - 1))
                last.then_inc(table_up, 1)

            def shared_in(k):
                b, c = k // IC, k % IC
                gate, up = SH_BANKS[k]
                if k == 0:
                    pe.wait_ge(sh_lo_done, 1)
                    pe.wait_ge(lg_done, B - 2)
                    pe.wait_ge(xfT_done, B - 2)
                elif k <= 2:
                    pe.wait_ge(p_done, NT)
                    pe.wait_ge(pT_done, NT)
                else:
                    pe.wait_ge(shhid_done, k - 1)
                if c == 0:
                    pe.wait_ge(xf_split, b + 1)
                cg, cu = slice(c * P, (c + 1) * P), slice(I + c * P, I + (c + 1) * P)
                split_product(gate[:, :], sh_gu_hi[:, cg], sh_gu_lo[:, cg], xf_hi[:, b, :], xf_lo[:, b, :]).then_inc(shg_up, 1)
                split_product(up[:, :], sh_gu_hi[:, cu], sh_gu_lo[:, cu], xf_hi[:, b, :], xf_lo[:, b, :]).then_inc(shu_up, 1)

            def shared_out(b):
                pe.wait_ge(shhid_done, IC * (b + 1))
                pe.wait_ge(shd_done, b + 1)
                if b >= 2:
                    pe.wait_ge(base_done, b - 1)
                else:
                    pe.wait_ge(x1_done, NT)
                for t in range(T):
                    for c in range(IC):
                        last = pe.matmul(O[b % 2][:, t * H:(t + 1) * H], sh_hid[:, (IC * b + c) % 4, t * P:(t + 1) * P], sh_down_gb[:, b, c, :],
                                         start=(c == 0), stop=(c == IC - 1))
                last.then_inc(shd_up, 1)

            pe.wait_ge(ld_vec, 16)
            pe.wait_ge(c_done, 1)
            pe.transpose(M[0][:, 0:8], vec_rows[:, :], ident[0:8, 0:8]).then_inc(vec_up, 1)
            pe.wait_ge(silu_done, 1)
            pe.wait_ge(ld_wmod, 16)
            for j in range(2):
                last = pe.matmul(M[1][:, j * B:(j + 1) * B], wmod_sb[:, j * H:(j + 1) * H], silu_c[:, :], start=True, stop=True)
            last.then_inc(modc_up, 1)
            pe.matmul(PT[0][0:B, :], silu_c[:, :], wmod_sb[:, 2 * H:6 * H], start=True, stop=True).then_inc(modr_up, 1)
            rows_T(0)
            pe.wait_ge(ld_wqkv, 16)
            q_product(0)
            k_product(0)
            pe.wait_ge(modr_done, 4)
            pe.wait_ge(c_done, CONSTS)
            for b in range(B):
                bank = (PT[1], O[1], S[0], S[1])[b]
                if b == 0:
                    for c in range(B):
                        last = pe.matmul(O[0][:, c * H:(c + 1) * H], pick_b[:, c, :], mod_rows[:, 0, :], start=True, stop=True)
                    last.then_inc(ga_up, 1)
                pe.matmul(bank[:, :], pick_b[:, b, :], mod_rows[:, 1:5, :], start=True, stop=True).then_inc(row_up, 1)
            pe.wait_ge(wv_done, 1)
            v_product(0)
            pe.wait_ge(bc_done, B)
            pe.wait_ge(modr_raw, 1)
            scores(0)
            scores(1)
            for b in range(B):
                n = T * b
                nxt = b + 1 < B
                probs_up(n)
                scores(n + 2)
                attend(n)
                probs_up(n + 1)
                if nxt:
                    rows_T(b + 1)
                scores(n + 3)
                attend(n + 1)
                probs_up(n + 2)
                if nxt:
                    q_product(b + 1)
                else:
                    shared_in(0)
                attend(n + 2)
                if nxt:
                    k_product(b + 1)
                probs_up(n + 3)
                if nxt:
                    v_product(b + 1)
                else:
                    shared_in(1)
                attend(n + 3)
                if b >= 1:
                    if b == 1:
                        pe.wait_ge(ld_router, 16)
                    z_T(b - 1)
                if nxt:
                    scores(n + T)
                if b >= 1:
                    logits(b - 1)
                if nxt:
                    scores(n + T + 1)
            shared_in(2)
            shared_in(3)
            shared_out(0)
            z_T(B - 1)
            logits(B - 1)
            shared_in(4)
            shared_out(1)
            rank_product()
            shared_in(5)
            shared_in(6)
            shared_out(2)
            table_product()
            shared_in(7)
            shared_out(3)

            pe.wait_ge(sexp_done, 1)
            _, expert = nc.values_load_multi_w_load_instructions(
                slot_exp_i[0:1, :], engines=(mybir.EngineType.PE,), min_val=0, max_val=E - 1,
                skip_runtime_bounds_check_because="min with E - 1 of a sum of comparisons")
            pe.wait_ge(w_lo_done, B)
            pe.wait_ge(ld_down, 16)

            def slot_T(s):
                pe.wait_ge(gathered[s], 16)
                if s >= 2:
                    pe.wait_ge(xs_done, s - 1)
                else:
                    pe.wait_ge(table_read, 1)
                pe.transpose(M[s % 2][:, 0:P], zg[:, s % RING, 0:H], ident[:, :]).then_inc(xs_up, 1)

            def slot_in(s):
                pe.wait_ge(xlo_done, s + 1)
                if s >= 2:
                    pe.wait_ge(sh_done, s - 1)
                else:
                    pe.wait_ge(shhid_done, IC * B)
                cols_e = bass.ds(expert[s] * (2 * I), 2 * I)
                split_product(S[s % 2][:, :], xs_hi[:, s % 2, :], xs_lo[:, s % 2, :], w_gu_hi[:, cols_e], w_gu_lo[:, cols_e]
                              ).then_inc(gu_up, 1)

            def slot_hid_T(s):
                pe.wait_ge(sh_done, s + 1)
                if s >= 2:
                    pe.wait_ge(ht_done, s - 1)
                transposes(PT[s % 2], lambda c: sl_hid[:, s % 2, c * P:(c + 1) * P], IC).then_inc(ht_up, 1)

            def slot_out(s):
                pe.wait_ge(ht_done, s + 1)
                if s >= 2:
                    pe.wait_ge(y_done, s - 1)
                else:
                    pe.wait_ge(base_done, B)
                for c in range(IC):
                    last = pe.matmul(O[s % 2][:, 0:H], sl_hidT[:, s % 2, c, :],
                                     w_down_sb[:, bass.ds(expert[s] * (IC * H) + c * H, H)], start=(c == 0), stop=(c == IC - 1))
                last.then_inc(y_up, 1)

            slot_T(0)
            for s in range(NS + 2):
                if s + 1 < NS:
                    slot_T(s + 1)
                if s < NS:
                    slot_in(s)
                if s >= 2:
                    slot_out(s - 2)
                if 1 <= s <= NS:
                    slot_hid_T(s - 1)


def kernel(**inputs):
    import numpy as np
    import concourse.bacc as bacc
    from concourse.bass_utils import run_bass_kernel_spmd

    a = {k.removeprefix("L0_"): np.asarray(v) for k, v in inputs.items()}
    side_by_side = lambda g, u, axis: np.concatenate([g, u], axis=axis)
    arrays = {
        "x": a["attn_x"].reshape(B * L, H),
        "vecs": np.concatenate([np.stack([a["attn_bq"], a["attn_bk"], a["ffn_ln_w"], a["ffn_ln_b"]]), a["c"]]),
        "bv": a["attn_bv"],
        "wmod": a["wmod"],
        "wqkv": np.stack([a["attn_Wq"].T, a["attn_Wk"].T, a["attn_Wv"].T], axis=1),
        "router_w": a["ffn_router_w"],
        "w_gu": side_by_side(a["ffn_gate_w"], a["ffn_up_w"], 2).transpose(1, 0, 2).reshape(H, E * 2 * I),
        "w_down": a["ffn_down_w"].reshape(E, IC, P, H).transpose(2, 0, 1, 3).reshape(P, E * IC * H),
        "sh_gu": side_by_side(a["ffn_sh_gate"], a["ffn_sh_up"], 1),
        "sh_down": a["ffn_sh_down"].reshape(IC, P, H).transpose(1, 0, 2),
    }
    arrays = {f"in_{k}": np.ascontiguousarray(v) for k, v in arrays.items()}
    nc = bacc.Bacc("TRN2", target_bir_lowering=False, num_devices=1)
    args = [nc.dram_tensor(k, v.shape, mybir.dt.from_np(v.dtype), kind="ExternalInput").ap() for k, v in arrays.items()]
    out = nc.dram_tensor("out_0", (NS * P, H), F32, kind="ExternalOutput").ap()
    adaln_block(nc, *args, out)
    r = run_bass_kernel_spmd(nc, [arrays], core_ids=[0])
    return r.results[0]["out_0"][:B * L].reshape(B, L, H)
```

```python
from contextlib import ExitStack

import concourse.bass as bass
from concourse import mybir

F32 = mybir.dt.float32
BF16 = mybir.dt.bfloat16
F32R = mybir.dt.float32r
I32 = mybir.dt.int32
ALU = mybir.AluOpType
ACT = mybir.ActivationFunctionType
AX_X = mybir.AxisListType.X

P = 128
B = 4
L = 512
H = 128
T = L // P
NT = B * T
E = 8
I = 256
IC = I // P
NS = NT + E - 1
ZW = 2 * H + 2
REGION = B * L + P
SPARE = E + NS - NT
EPS = 1e-5
LOWEST = -3.3895313892515355e38
RSQRT_MAGIC = float(0x5F3759DF)
ROUND_P = 1.5 * (1 << 23) * P


class Steps:

    def __init__(self, eng, sem):
        self.eng, self.sem, self.count = eng, sem, 0

    def then(self, instruction):
        instruction.then_inc(self.sem, 1)
        self.count += 1

    def done(self):
        self.eng.wait_ge(self.sem, self.count)

    def chain(self, instruction):
        self.then(instruction)
        self.done()


def adaln_block(nc, x, vecs, bv, wmod, wqkv, router_w, w_gu, w_down, sh_gu, sh_down, out):
    regions = nc.dram_tensor("regions", [E * REGION + (SPARE - E) * P, ZW], F32).ap()
    mod_dram = nc.dram_tensor("mod_dram", [B, 5 * H], F32).ap()

    ctx = ExitStack()
    with ctx:
        def sb(name, shape, dt=F32):
            return ctx.enter_context(nc.sbuf_tensor(name, shape, dt))

        def bank(name):
            return ctx.enter_context(nc.psum_tensor(name, [P, 512], F32))

        def sem(name):
            return ctx.enter_context(nc.semaphore(name))

        xs = sb("xs", [P, NT, H])
        vec_rows = sb("vec_rows", [8, H])
        bv_rows = sb("bv_rows", [B, H])
        wmod_sb = sb("wmod_sb", [P, 6 * H])
        wqkv_sb = sb("wqkv_sb", [P, 3, H])
        router_sb = sb("router_sb", [P, E])
        w_gu_sb = sb("w_gu_sb", [P, E * 2 * I])
        w_gu_hi = sb("w_gu_hi", [P, E * 2 * I], F32R)
        w_gu_lo = sb("w_gu_lo", [P, E * 2 * I], F32R)
        w_down_sb = sb("w_down_sb", [P, E * IC * H])
        sh_gu_sb = sb("sh_gu_sb", [P, 2 * I])
        sh_gu_hi = sb("sh_gu_hi", [P, 2 * I], F32R)
        sh_gu_lo = sb("sh_gu_lo", [P, 2 * I], F32R)
        sh_down_sb = sb("sh_down_sb", [P, IC, H])
        ident = sb("ident", [P, P])
        ident_b = sb("ident_b", [P, P], BF16)
        mask_diag = sb("mask_diag", [P, P], BF16)
        not_before = sb("not_before", [P, P], BF16)
        ones_b = sb("ones_b", [P, P], BF16)
        iota_e = sb("iota_e", [P, E])
        iota_e8 = sb("iota_e8", [P, E])
        iota_s = sb("iota_s", [P, NS])
        region_at = sb("region_at", [P, E])
        same_e = sb("same_e", [P, E, T])
        ones_e = sb("ones_e", [P, E])
        warm = sb("warm", [P, 512], BF16)
        no_token = sb("no_token", [P, ZW + SPARE - 1])
        cols = sb("cols", [P, 8])
        bq_h = sb("bq_h", [P, 1])
        silu_c = sb("silu_c", [P, B])
        exp_first = sb("exp_first", [P, 1])
        shift_a = sb("shift_a", [P, B])
        scale_a = sb("scale_a", [P, B])
        mod_raw = sb("mod_raw", [B, 4, H])
        gate_sign = sb("gate_sign", [B, 2, H])
        gate_abs = sb("gate_abs", [B, 2, H])
        gate_half = sb("gate_half", [B, 2, H])
        mod_rows = sb("mod_rows", [B, 5, H])
        bc = sb("bc", [P, B, 5, H])
        wv_ga = sb("wv_ga", [P, B, H])
        sh_down_gb = sb("sh_down_gb", [P, B, IC, H])
        st1 = sb("st1", [P, NT, 6])
        mv1 = sb("mv1", [P, NT, 2])
        v1 = sb("v1", [P, NT])
        t1 = sb("t1", [P, NT])
        r1 = sb("r1", [P, NT])
        root_q = sb("root_q", [P, NT])
        nmr1 = sb("nmr1", [P, NT])
        normed = sb("normed", [P, T, H])
        hT = sb("hT", [P, L])
        qT = sb("qT", [P, L])
        kT = sb("kT", [P, L])
        v_sb = sb("v_sb", [P, 2, T, H])
        neg_max = sb("neg_max", [P, NT])
        probs = sb("probs", [P, 2, L])
        prob_sum = sb("prob_sum", [P, NT])
        prob_inv = sb("prob_inv", [P, NT])
        probsT = sb("probsT", [P, 2, L])
        st2 = sb("st2", [P, NT, 6])
        mv2 = sb("mv2", [P, NT, 2])
        v2 = sb("v2", [P, NT])
        t2 = sb("t2", [P, NT])
        r2 = sb("r2", [P, NT])
        h2u = sb("h2u", [P, T, H])
        h2 = sb("h2", [P, T, H])
        st3 = sb("st3", [P, NT, 6])
        mv3 = sb("mv3", [P, NT, 2])
        v3 = sb("v3", [P, NT])
        t3 = sb("t3", [P, NT])
        r3 = sb("r3", [P, NT])
        zw = sb("zw", [P, NS, ZW])
        gh2 = sb("gh2", [P, T, H])
        xfT = sb("xfT", [P, L])
        xf_hi = sb("xf_hi", [P, B, L], F32R)
        xf_lo = sb("xf_lo", [P, B, L], F32R)
        top = sb("top", [P, NT])
        tanh_top = sb("tanh_top", [P, NT])
        is_top = sb("is_top", [P, NT, E])
        cand = sb("cand", [P, NT, E])
        first = sb("first", [P, NT])
        region = sb("region", [P, NT])
        onehot = sb("onehot", [P, B, E, T], BF16)
        seen = sb("seen", [P, B, E, T], BF16)
        seen_all = sb("seen_all", [P, B + 1, E], BF16)
        rank_of = sb("rank_of", [P, NT, E])
        rank = sb("rank", [P, NT])
        place = sb("place", [P, NT], I32)
        count_up = sb("count_up", [P, E])
        slots_128 = sb("slots_128", [P, E])
        end_128 = sb("end_128", [P, E])
        behind = sb("behind", [P, E], I32)
        slot_past = sb("slot_past", [P, NS, E])
        past_128 = sb("past_128", [P, NS, E])
        slot_exp = sb("slot_exp", [P, NS])
        start_128 = sb("start_128", [P, NS])
        slot_at = sb("slot_at", [P, NS])
        slot_exp_i = sb("slot_exp_i", [P, NS], I32)
        slot_row_i = sb("slot_row_i", [P, NS], I32)
        sh_silu = sb("sh_silu", [P, 2, L])
        sh_up = sb("sh_up", [P, 2, L])
        sh_hid = sb("sh_hid", [P, 4, L])
        xsT = sb("xsT", [P, 3, P])
        xs_hi = sb("xs_hi", [P, 3, P], F32R)
        xs_lo = sb("xs_lo", [P, 3, P], F32R)
        sl_hidT = sb("sl_hidT", [P, 3, IC, P])
        y_sl = w_gu_sb[:, 0:NS * H].rearrange("p (s h) -> p s h", s=NS)
        sl_silu = w_gu_sb[:, NS * H:NS * H + 2 * I].rearrange("p (k i) -> p k i", k=2)
        sl_hid = w_gu_sb[:, NS * H + 2 * I:NS * H + 4 * I].rearrange("p (k i) -> p k i", k=2)

        S = [bank("S0"), bank("S1")]
        PT = [bank("PT0"), bank("PT1")]
        O = [bank("O0"), bank("O1")]
        M = [bank("M0"), bank("M1")]

        ld_x = [sem(f"ld_x{b}") for b in range(B)]
        ld_vec, ld_bv, ld_wmod, ld_wqkv = sem("ld_vec"), sem("ld_bv"), sem("ld_wmod"), sem("ld_wqkv")
        ld_router, ld_sh_gu, ld_sh_down = sem("ld_router"), sem("ld_sh_gu"), sem("ld_sh_down")
        ld_gu, ld_down = sem("ld_gu"), sem("ld_down")
        c_set = sem("c_set")
        c_done = sem("c_done")
        vec_up, cols_done, silu_done = sem("vec_up"), sem("cols_done"), sem("silu_done")
        modc_up, modc_done = sem("modc_up"), sem("modc_done")
        modr_up, modr_raw, modr_done = sem("modr_up"), sem("modr_raw"), sem("modr_done")
        mod_stored, wv_done = sem("mod_stored"), sem("wv_done")
        bc_in = [sem(f"bc_in{b}") for b in range(B)]
        shd_done, gate_copied = sem("shd_done"), sem("gate_copied")
        st1_done, mv1_done, r1_done, norm_done = sem("st1_done"), sem("mv1_done"), sem("r1_done"), sem("norm_done")
        nT_up, hT_done = sem("nT_up"), sem("hT_done")
        q_up, qT_done, k_up, kT_done, v_up, v_done = (sem(n) for n in ("q_up", "qT_done", "k_up", "kT_done", "v_up", "v_done"))
        s_up, max_done, p_done = sem("s_up"), sem("max_done"), sem("p_done")
        pT_up, pT_done, o_up, x1_done = sem("pT_up"), sem("pT_done"), sem("o_up"), sem("x1_done")
        xres_done, inv_done = sem("xres_done"), sem("inv_done")
        st2_done, mv2_done, h2u_done, h2_done = sem("st2_done"), sem("mv2_done"), sem("h2u_done"), sem("h2_done")
        st3_done, mv3_done, z_done, w_done = sem("st3_done"), sem("mv3_done"), sem("z_done"), sem("w_done")
        gh2_done, xb_done = sem("gh2_done"), sem("xb_done")
        zT_up, xfT_done, xf_split, lg_up, lg_done = sem("zT_up"), sem("xfT_done"), sem("xf_split"), sem("lg_up"), sem("lg_done")
        xf_hi_done, w_hi_done, w_lo_done, sh_hi_done, sh_lo_done = (sem(n) for n in ("xf_hi_done", "w_hi_done", "w_lo_done", "sh_hi_done", "sh_lo_done"))
        top_done, tanh_done, hot_done, seen_done = sem("top_done"), sem("tanh_done"), sem("hot_done"), sem("seen_done")
        total_done, rank_up, rank_read, place_done = sem("total_done"), sem("rank_up"), sem("rank_read"), sem("place_done")
        placed, padded, dummy_stored = sem("placed"), sem("padded"), sem("dummy_stored")
        behind_done, sexp_done, srow_done = sem("behind_done"), sem("sexp_done"), sem("srow_done")
        shg_up, shu_up, shsilu_done = sem("shg_up"), sem("shu_up"), sem("shsilu_done")
        shhid_done = [sem(f"shhid_done{k}") for k in range(IC * B)]
        shup_done = sem("shup_done")
        shd_up, base_done, base_stored = sem("shd_up"), sem("base_done"), sem("base_stored")
        slot_in_sem = [sem(f"slot_in{s}") for s in range(NS)]
        xs_up, xs_done, xhi_done, xlo_done = sem("xs_up"), sem("xs_done"), sem("xhi_done"), sem("xlo_done")
        gu_up, ss_done, sh_done = sem("gu_up"), sem("ss_done"), sem("sh_done")
        ht_up, ht_done, y_up, y_done = sem("ht_up"), sem("ht_done"), sem("y_up"), sem("y_done")
        scattered = sem("scattered")
        dve_step, route_step = sem("dve_step"), sem("route_step")

        x_v = x.rearrange("(b p t) h -> b p t h", p=P, t=T)
        out_v = out[0:B * L, :].rearrange("(b p t) h -> b p t h", p=P, t=T)
        WARM = (4, 5, 4, 3, 0, 6, 2, 3, 3)
        CONSTS = 13
        WC = E * 2 * I // B
        SH_BANKS = [M, S, PT, S, PT, S, PT, S]

        def tiles(buf, b):
            return buf[:, T * b:T * b + T]

        def chunks_beside(b):
            return [2 * b - 2, 2 * b - 1] if 1 <= b <= B // 2 else []

        def rank_psum(b):
            return O[0][:, H:H + T * E] if b < B - 2 else M[1][:, 0:T * E]

        def over(ap, shape):
            return ap.broadcast_to(shape)

        block = ctx.enter_context(nc.Block())

        @block.sync
        def _(sp):
            sp.dma_start(vec_rows[:, :], vecs).then_inc(ld_vec, 16)
            sp.dma_start(tiles(xs, 0), x_v[0]).then_inc(ld_x[0], 16)
            sp.dma_start(wmod_sb[:, :], wmod).then_inc(ld_wmod, 16)
            sp.dma_start(wqkv_sb[:, :, :], wqkv).then_inc(ld_wqkv, 16)
            sp.dma_start(bv_rows[:, :], bv.partition_broadcast(B)).then_inc(ld_bv, 16)
            for b in range(1, B):
                sp.dma_start(tiles(xs, b), x_v[b]).then_inc(ld_x[b], 16)
            sp.dma_start(router_sb[:, :], router_w).then_inc(ld_router, 16)
            sp.dma_start(sh_gu_sb[:, :], sh_gu).then_inc(ld_sh_gu, 16)
            sp.dma_start(sh_down_sb[:, :, :], sh_down).then_inc(ld_sh_down, 16)
            sp.wait_ge(modr_done, 4)
            sp.dma_start(mod_dram, mod_rows[:, :, :].rearrange("b j h -> b (j h)")).then_inc(mod_stored, 16)
            sp.wait_ge(mod_stored, 16)
            for b in range(B):
                sp.dma_start(bc[:, b].rearrange("p j h -> p (j h)"), mod_dram[b].partition_broadcast(P)).then_inc(bc_in[b], 16)
            sp.dma_start(w_gu_sb[:, :], w_gu).then_inc(ld_gu, 16)
            sp.dma_start(w_down_sb[:, :], w_down).then_inc(ld_down, 16)
            sp.wait_ge(ld_down, 16)
            sp.dma_start(out[B * L:, :].rearrange("(p j) h -> p (j h)", p=P), w_down_sb[:, 0:SPARE * H]).then_inc(dummy_stored, 16)
            sp.wait_ge(c_done, CONSTS)
            for k in range(E, SPARE):
                at = E * REGION + (k - E) * P
                sp.dma_start(regions[at:at + P, :], no_token[:, k:k + ZW]).then_inc(padded, 16)

            def store_base(b):
                sp.wait_ge(base_done, b + 1)
                sp.dma_start(out_v[b], tiles(xs, b)).then_inc(base_stored, 16)

            store_base(0)
            sp.wait_ge(behind_done, 1)
            _, behind_e = nc.values_load_multi_w_load_instructions(
                behind[0:1, :], engines=(mybir.EngineType.SP,), min_val=0, max_val=E * REGION - P,
                skip_runtime_bounds_check_because="an expert has at most B L tokens")
            for e in range(E):
                sp.dma_start(regions[bass.ds(behind_e[e], P), :], no_token[:, e:e + ZW]).then_inc(padded, 16)
            sp.wait_ge(srow_done, 1)
            _, slot_row = nc.values_load_multi_w_load_instructions(
                slot_row_i[0:1, :], engines=(mybir.EngineType.SP,), min_val=0, max_val=E * REGION + (SPARE - E - 1) * P,
                skip_runtime_bounds_check_because="a slot's region and its place there")
            sp.wait_ge(padded, 16 * SPARE)
            sp.wait_ge(placed, 16 * NT)
            for s in range(NS):
                sp.dma_start(zw[:, s, :], regions[bass.ds(slot_row[s], P), :]).then_inc(slot_in_sem[s], 16)
                if 5 <= s < 5 + B - 1:
                    store_base(s - 4)
            sp.wait_ge(base_stored, 16 * B)
            sp.wait_ge(scattered, 16 * NS)

        @block.gpsimd
        def _(pool):
            def hot(buf, fill):
                pool.affine_select(out=buf[:, :], in_=buf[:, :], pattern=[[-1, P]], base=0, channel_multiplier=1,
                                   compare_op=ALU.not_equal, fill=fill).then_inc(c_done, 1)

            def ramp(buf, pattern, base=0, channel=0):
                pool.iota(buf, pattern=pattern, base=base, channel_multiplier=channel,
                          allow_small_or_imprecise_dtypes=True).then_inc(c_done, 1)

            pool.memset(warm[:, :], 0.0).then_inc(c_set, 1)
            pool.memset(ident[:, :], 0.0).then_inc(c_set, 1)
            pool.memset(mask_diag[:, :], 0.0).then_inc(c_set, 1)
            pool.memset(ident_b[:, :], 0.0).then_inc(c_set, 1)
            pool.memset(not_before[:, :], -1.0).then_inc(c_set, 1)
            pool.memset(no_token[:, :], 0.0).then_inc(c_set, 1)
            pool.memset(same_e[:, :, :], 1.0).then_inc(c_set, 1)
            pool.wait_ge(c_set, 2)
            hot(ident, 1.0)
            pool.wait_ge(c_set, 7)
            hot(mask_diag, LOWEST)
            hot(ident_b, 1.0)
            pool.memset(ones_b[:, :], 1.0).then_inc(c_done, 1)
            pool.memset(ones_e[:, :], 1.0).then_inc(c_done, 1)
            ramp(iota_e[:, :], [[1, E]])
            ramp(iota_e8[:, :], [[1, E]], base=-E)
            ramp(iota_s[:, :], [[P, NS]])
            ramp(region_at[:, :], [[REGION, E]])
            ramp(zw[:, 0:NT, ZW - 1].bitcast(I32).rearrange("p (b t) -> p b t", b=B), [[L, B], [1, T]], channel=T)
            ramp(no_token[:, ZW - 1:].bitcast(I32), [[P, SPARE]], base=B * L, channel=1)
            pool.affine_select(out=not_before[:, :], in_=not_before[:, :], pattern=[[-1, P]], base=0, channel_multiplier=1,
                               compare_op=ALU.is_ge, fill=0.0).then_inc(c_done, 1)
            pool.affine_select(out=same_e[:, :, :], in_=same_e[:, :, :], pattern=[[0, E], [1, T]], base=0,
                               channel_multiplier=0, compare_op=ALU.is_gt, fill=0.0).then_inc(c_done, 1)

            def residual(b):
                pool.wait_ge(norm_done, T * (b + 1))
                pool.wait_ge(bc_in[b], 16)
                pool.tensor_tensor(tiles(xs, b), tiles(xs, b), over(bc[:, b, 4:5, :], [P, T, H]),
                                   ALU.add).then_inc(xres_done, 1)

            def gates(b):
                pool.wait_ge(bc_in[b], 16)
                pool.tensor_tensor(sh_down_gb[:, b], sh_down_sb[:, :, :], over(bc[:, b, 1:2, :], [P, IC, H]),
                                   ALU.mult).then_inc(shd_done, 1)
                pool.tensor_copy(tiles(zw, b)[:, :, H + 1:2 * H + 1], over(bc[:, b, 1:2, :], [P, T, H])).then_inc(gate_copied, 1)

            def base_rows(b):
                pool.wait_ge(h2_done, T * (b + 1))
                if b >= 1:
                    pool.wait_ge(xb_done, b)
                pool.tensor_tensor(gh2[:, :, :], h2[:, :, :], over(bc[:, b, 1:2, :], [P, T, H]), ALU.mult).then_inc(gh2_done, 1)
                pool.wait_ge(gh2_done, b + 1)
                pool.tensor_tensor(tiles(xs, b), gh2[:, :, :], tiles(xs, b), ALU.add).then_inc(xb_done, 1)

            def split_rows(b):
                pool.wait_ge(xf_hi_done, b + 1)
                pool.tensor_tensor(xf_lo[:, b, :], xfT[:, :], xf_hi[:, b, :].bitcast(F32), ALU.subtract).then_inc(xf_split, 1)

            def split_weights(b):
                c = slice(WC * b, WC * (b + 1))
                pool.wait_ge(w_hi_done, b + 1)
                pool.tensor_tensor(w_gu_lo[:, c], w_gu_sb[:, c], w_gu_hi[:, c].bitcast(F32), ALU.subtract).then_inc(w_lo_done, 1)

            def place_rows(b, lo=0, hi=T):
                pool.wait_ge(place_done, b + 1)
                pool.wait_ge(w_done, b + 1)
                for n in range(T * b + lo, T * b + hi):
                    pool.indirect_dma_start(out=regions, out_offset=bass.IndirectOffsetOnAxis(ap=place[:, n:n + 1], axis=0),
                                            in_=zw[:, n, :], in_offset=None).then_inc(placed, 16)

            def shared_hidden(k):
                pool.wait_ge(shsilu_done, k + 1)
                pool.wait_ge(shup_done, k + 1)
                if k >= 4:
                    pool.wait_ge(shd_up, (k - 4) // IC + 1)
                pool.tensor_tensor(sh_hid[:, k % 4, :], sh_silu[:, k % 2, :], sh_up[:, k % 2, :], ALU.mult).then_inc(shhid_done[k], 1)

            residual(0)
            pool.wait_ge(ld_sh_down, 16)
            gates(0)
            for b in range(B):
                if b + 1 < B:
                    residual(b + 1)
                    gates(b + 1)
                if b == 1:
                    pool.wait_ge(sh_hi_done, 1)
                    pool.tensor_tensor(sh_gu_lo[:, :], sh_gu_sb[:, :], sh_gu_hi[:, :].bitcast(F32), ALU.subtract).then_inc(sh_lo_done, 1)
                if b >= 1:
                    base_rows(b - 1)
                    if b == B - 1:
                        shared_hidden(0)
                        shared_hidden(1)
                        place_rows(b - 2, 0, 2)
                    elif b >= 2:
                        place_rows(b - 2)
                    for k in chunks_beside(b):
                        split_weights(k)
                    split_rows(b - 1)
            shared_hidden(2)
            shared_hidden(3)
            place_rows(B - 3, 2, T)
            place_rows(B - 2)
            place_rows(B - 1)
            base_rows(B - 1)
            pool.wait_ge(base_stored, 16 * B)
            pool.wait_ge(dummy_stored, 16)
            for s in range(NS):
                pool.wait_ge(y_done, s + 1)
                pool.indirect_dma_start(out=out, out_offset=bass.IndirectOffsetOnAxis(ap=zw[:, s, ZW - 1:].bitcast(I32), axis=0),
                                        in_=y_sl[:, s, :], in_offset=None, compute_op=ALU.add).then_inc(scattered, 16)

        @block.scalar
        def _(act):
            def norm1(b):
                act.wait_ge(r1_done, min(b + 1, 3))
                if b >= 1:
                    act.wait_ge(nT_up, b)
                for t in range(2 if b == 0 else T):
                    n = T * b + t
                    act.activation(normed[:, t, :], xs[:, n, :], ACT.Identity, bias=nmr1[:, n:n + 1],
                                   scale=r1[:, n:n + 1]).then_inc(norm_done, 1)

            def h_rows(b):
                act.wait_ge(nT_up, b + 1)
                act.activation(hT[:, :], M[0][:, :], ACT.Identity, bias=shift_a[:, b:b + 1],
                               scale=scale_a[:, b:b + 1]).then_inc(hT_done, 1)

            def q_rows(b):
                act.wait_ge(q_up, b + 1)
                act.activation(qT[:, :], M[1][:, :], ACT.Identity, bias=bq_h[:, 0:1], scale=1.0 / H).then_inc(qT_done, 1)

            def k_rows(b):
                act.wait_ge(k_up, b + 1)
                act.activation(kT[:, :], M[0][:, :], ACT.Identity, bias=cols[:, 1:2]).then_inc(kT_done, 1)

            def v_rows(b):
                act.wait_ge(v_up, b + 1)
                act.activation(v_sb[:, b % 2], M[1][:, :].rearrange("p (t h) -> p t h", t=T), ACT.Copy).then_inc(v_done, 1)

            def exps(n):
                act.wait_ge(max_done, n + 1)
                if n >= 2:
                    act.wait_ge(pT_up, n - 1)
                act.activation(probs[:, n % 2, :], S[n % 2][:, :], ACT.Exp, bias=neg_max[:, n:n + 1],
                               accum_out=prob_sum[:, n:n + 1]).then_inc(p_done, 1)

            def probs_T(n):
                act.wait_ge(pT_up, n + 1)
                if n >= 2:
                    act.wait_ge(o_up, n - 1)
                act.activation(probsT[:, n % 2, :], PT[n % 2][:, :], ACT.Copy).then_inc(pT_done, 1)

            def xf_rows(b):
                act.wait_ge(zT_up, b + 1)
                if b >= 1:
                    act.wait_ge(lg_up, b)
                    act.wait_ge(xf_split, b)
                act.activation(xfT[:, :], M[0][:, :], ACT.Identity, bias=cols[:, 3:4], scale=cols[:, 2:3]).then_inc(xfT_done, 1)

            def xf_hi_rows(b):
                act.wait_ge(xfT_done, b + 1)
                act.activation(xf_hi[:, b, :], xfT[:, :], ACT.Copy).then_inc(xf_hi_done, 1)

            def weights_hi(b):
                c = slice(WC * b, WC * (b + 1))
                if b == 0:
                    act.wait_ge(ld_gu, 16)
                act.activation(w_gu_hi[:, c], w_gu_sb[:, c], ACT.Copy).then_inc(w_hi_done, 1)

            def shared_silu(k):
                act.wait_ge(shg_up, k + 1)
                if k >= 2:
                    act.wait_ge(shhid_done[k - 2], 1)
                act.activation(sh_silu[:, k % 2, :], SH_BANKS[k][0][:, :], ACT.Silu).then_inc(shsilu_done, 1)

            def shared_up(k):
                act.wait_ge(shu_up, k + 1)
                if k >= 2:
                    act.wait_ge(shhid_done[k - 2], 1)
                act.activation(sh_up[:, k % 2, :], SH_BANKS[k][1][:, :], ACT.Copy).then_inc(shup_done, 1)

            def score_tanh(b):
                act.wait_ge(top_done, b + 1)
                act.activation(tiles(tanh_top, b), tiles(top, b), ACT.Tanh, scale=0.5).then_inc(tanh_done, 1)

            act.wait_ge(cols_done, 1)
            act.activation(silu_c[:, :], cols[:, 4:8], ACT.Silu).then_inc(silu_done, 1)
            act.wait_ge(silu_done, 1)
            act.activation(exp_first[:, :], silu_c[:, 0:1], ACT.Exp, scale=0.0)
            act.wait_ge(cols_done, 2)
            norm1(0)
            act.wait_ge(modc_done, 2)
            h_rows(0)
            q_rows(0)
            k_rows(0)
            norm1(1)
            exps(0)
            exps(1)
            v_rows(0)
            for b in range(B):
                n = T * b
                nxt = b + 1 < B
                probs_T(n)
                if nxt and b >= 1:
                    norm1(b + 1)
                exps(n + 2)
                probs_T(n + 1)
                if nxt:
                    h_rows(b + 1)
                exps(n + 3)
                if b >= 2:
                    score_tanh(b - 2)
                probs_T(n + 2)
                if nxt:
                    q_rows(b + 1)
                    for k in chunks_beside(b)[0:1]:
                        weights_hi(k)
                    k_rows(b + 1)
                else:
                    shared_silu(0)
                    shared_up(0)
                probs_T(n + 3)
                if nxt:
                    v_rows(b + 1)
                else:
                    shared_silu(1)
                    shared_up(1)
                for k in chunks_beside(b)[1:2] if nxt else []:
                    weights_hi(k)
                if b == 0:
                    act.wait_ge(ld_sh_gu, 16)
                    act.activation(sh_gu_hi[:, :], sh_gu_sb[:, :], ACT.Copy).then_inc(sh_hi_done, 1)
                if nxt:
                    exps(n + T)
                if b >= 1:
                    xf_rows(b - 1)
                if nxt:
                    exps(n + T + 1)
                if b >= 1:
                    xf_hi_rows(b - 1)
            shared_silu(2)
            shared_up(2)
            shared_silu(3)
            shared_up(3)
            shared_silu(4)
            score_tanh(B - 2)
            xf_rows(B - 1)
            xf_hi_rows(B - 1)
            shared_silu(5)
            score_tanh(B - 1)
            for k in range(6, 2 * B):
                shared_silu(k)
            def slot_x(s):
                act.wait_ge(xs_up, s + 1)
                if s >= 3:
                    act.wait_ge(xlo_done, s - 2)
                act.activation(xsT[:, s % 3, :], M[s % 2][:, 0:P], ACT.Identity, bias=cols[:, 3:4],
                               scale=cols[:, 2:3]).then_inc(xs_done, 1)

            slot_x(0)
            slot_x(1)
            act.wait_ge(w_lo_done, B)
            for s in range(NS + 1):
                if s < NS:
                    act.wait_ge(gu_up, s + 1)
                    if s >= 2:
                        act.wait_ge(sh_done, s - 1)
                    act.activation(sl_silu[:, s % 2, :], S[s % 2][:, 0:I], ACT.Silu,
                                   scale=zw[:, s, H:H + 1]).then_inc(ss_done, 1)
                if s + 2 < NS:
                    slot_x(s + 2)
                if s >= 1:
                    k = s - 1
                    act.wait_ge(ht_up, k + 1)
                    if k >= 3:
                        act.wait_ge(y_up, k - 2)
                    act.activation(sl_hidT[:, k % 3], PT[k % 2][:, 0:I].rearrange("p (c q) -> p c q", c=IC),
                                   ACT.Copy).then_inc(ht_done, 1)

        @block.vector
        def _(dve):
            small = Steps(dve, dve_step)
            routing = Steps(dve, route_step)

            def rsqrt(v, t, r, mv, lo, hi, done=None, between=()):
                v, t, r = v[:, lo:hi], t[:, lo:hi], r[:, lo:hi]
                q = root_q[:, lo:hi]
                between = list(between)

                def other():
                    if between:
                        between.pop(0)()

                small.then(dve.tensor_scalar(v, mv[:, lo:hi, 1], EPS, None, ALU.add))
                other()
                small.done()
                small.then(dve.tensor_scalar(r.bitcast(I32), v.bitcast(I32), -0.5, RSQRT_MAGIC, ALU.mult, ALU.add))
                other()
                small.done()
                small.then(dve.tensor_tensor(t, r, r, ALU.mult))
                other()
                small.done()
                small.then(dve.scalar_tensor_tensor(out=t, in0=t, scalar=-0.5, in1=v, op0=ALU.mult, op1=ALU.mult))
                other()
                small.done()
                small.then(dve.scalar_tensor_tensor(out=r, in0=t, scalar=1.5, in1=r, op0=ALU.add, op1=ALU.mult))
                other()
                small.done()
                small.then(dve.tensor_tensor(t, r, r, ALU.mult))
                small.then(dve.tensor_scalar(q, r, 0.375, None, ALU.mult))
                other()
                small.done()
                small.then(dve.tensor_tensor(t, t, v, ALU.mult))
                other()
                small.done()
                small.then(dve.scalar_tensor_tensor(out=t, in0=t, scalar=-10.0 / 3.0, in1=t, op0=ALU.add, op1=ALU.mult))
                other()
                small.done()
                small.then(dve.scalar_tensor_tensor(out=r, in0=t, scalar=5.0, in1=q, op0=ALU.add, op1=ALU.mult))
                while between:
                    other()
                small.done()

            def norm1_stats(lo, hi, k, between=()):
                for n in range(lo, hi):
                    dve.bn_stats(st1[:, n, :], xs[:, n, :]).then_inc(st1_done, 1)
                for n in range(lo, hi):
                    dve.wait_ge(st1_done, n + 1)
                    dve.bn_aggr(mv1[:, n, :], st1[:, n, :]).then_inc(mv1_done, 1)
                dve.wait_ge(mv1_done, hi)
                rsqrt(v1, t1, r1, mv1, lo, hi, between=between)
                dve.scalar_tensor_tensor(out=nmr1[:, lo:hi], in0=mv1[:, lo:hi, 0], scalar=-1.0, in1=r1[:, lo:hi],
                                         op0=ALU.mult, op1=ALU.mult).then_inc(r1_done, 1)

            def score_max(n):
                dve.wait_ge(s_up, n + 1)
                dve.tensor_reduce(neg_max[:, n:n + 1], S[n % 2][:, :], AX_X, ALU.max, negate=True).then_inc(max_done, 1)

            def invert_sum(n):
                dve.wait_ge(p_done, n + 1)
                dve.reciprocal(prob_inv[:, n:n + 1], prob_sum[:, n:n + 1]).then_inc(inv_done, 1)

            def attention_out(n):
                dve.wait_ge(inv_done, n + 1)
                dve.wait_ge(xres_done, n // T + 1)
                dve.wait_ge(o_up, n + 1)
                dve.scalar_tensor_tensor(out=xs[:, n, :], in0=O[n % 2][:, 0:H], scalar=prob_inv[:, n:n + 1],
                                         in1=xs[:, n, :], op0=ALU.mult, op1=ALU.add).then_inc(x1_done, 1)
                if n % T >= 1:
                    norm2_stats(n - 1)
                if n % T >= 2:
                    norm2_aggr(n - 2)

            def norm2_stats(n):
                dve.wait_ge(x1_done, n + 1)
                dve.bn_stats(st2[:, n, :], xs[:, n, :]).then_inc(st2_done, 1)

            def norm2_aggr(n):
                dve.wait_ge(st2_done, n + 1)
                dve.bn_aggr(mv2[:, n, :], st2[:, n, :]).then_inc(mv2_done, 1)

            def norm2_centre(n):
                b, t = n // T, n % T
                dve.scalar_tensor_tensor(out=h2u[:, t, :], in0=xs[:, n, :], scalar=mv2[:, n, 0:1], in1=bc[:, b, 3, :],
                                         op0=ALU.subtract, op1=ALU.mult).then_inc(h2u_done, 1)

            def norm2(b, between=(), before=()):
                lo, hi = T * b, T * b + T
                norm2_stats(hi - 1)
                norm2_aggr(hi - 2)
                norm2_aggr(hi - 1)
                dve.wait_ge(mv2_done, hi)
                if b >= 1:
                    dve.wait_ge(h2_done, lo)
                rsqrt(v2, t2, r2, mv2, lo, hi,
                      between=list(before) + [lambda n=n: norm2_centre(n) for n in range(lo, hi)] + list(between))
                if b >= 1:
                    dve.wait_ge(gh2_done, b)
                for n in range(lo, hi):
                    dve.wait_ge(h2u_done, n + 1)
                    dve.scalar_tensor_tensor(out=h2[:, n - lo, :], in0=h2u[:, n - lo, :], scalar=r2[:, n:n + 1], in1=bc[:, b, 2, :],
                                             op0=ALU.mult, op1=ALU.add).then_inc(h2_done, 1)

            def norm3(b, between=(), beside=()):
                beside = list(beside)
                lo, hi = T * b, T * b + T
                for n in range(lo, hi):
                    dve.wait_ge(h2_done, n + 1)
                    dve.bn_stats(st3[:, n, :], h2[:, n - lo, :]).then_inc(st3_done, 1)
                for n in range(lo, hi):
                    dve.wait_ge(st3_done, n + 1)
                    dve.bn_aggr(mv3[:, n, :], st3[:, n, :]).then_inc(mv3_done, 1)
                dve.wait_ge(mv3_done, hi)
                rsqrt(v3, t3, r3, mv3, lo, hi, between=between)
                for n in range(lo, hi):
                    dve.tensor_scalar(zw[:, n, 0:H], h2[:, n - lo, :], mv3[:, n, 0:1], r3[:, n:n + 1],
                                      ALU.subtract, ALU.mult).then_inc(z_done, 1)
                    if beside:
                        beside.pop(0)()

            def shared_hidden(k):
                dve.wait_ge(shsilu_done, k + 1)
                dve.wait_ge(shu_up, k + 1)
                if k >= 4:
                    dve.wait_ge(shd_up, (k - 4) // IC + 1)
                dve.tensor_tensor(sh_hid[:, k % 4, :], sh_silu[:, k % 2, :], SH_BANKS[k][1][:, :], ALU.mult).then_inc(shhid_done[k], 1)

            def shared_out(b):
                dve.wait_ge(shd_up, b + 1)
                dve.wait_ge(xb_done, b + 1)
                dve.tensor_tensor(tiles(xs, b), O[b % 2][:, :].rearrange("p (t h) -> p t h", t=T), tiles(xs, b),
                                  ALU.add).then_inc(base_done, 1)

            def routes(b):
                lg = M[1][:, 0:T * E].rearrange("p (t e) -> p t e", t=T)
                hot_b, seen_b = onehot[:, b], seen[:, b]

                def largest():
                    dve.wait_ge(lg_up, b + 1)
                    dve.tensor_reduce(tiles(top, b), lg, AX_X, ALU.max).then_inc(top_done, 1)

                def where():
                    dve.wait_ge(top_done, b + 1)
                    dve.tensor_tensor(tiles(is_top, b), lg, over(tiles(top, b).unsqueeze(2), [P, T, E]), ALU.is_equal
                                      ).then_inc(lg_done, 1)

                def candidates():
                    dve.wait_ge(lg_done, b + 1)
                    routing.then(dve.scalar_tensor_tensor(out=tiles(cand, b), in0=tiles(is_top, b), scalar=-float(E),
                                                          in1=over(iota_e[:, :].unsqueeze(1), [P, T, E]), op0=ALU.mult, op1=ALU.add))

                def lowest():
                    routing.done()
                    routing.then(dve.tensor_reduce(tiles(first, b), tiles(cand, b), AX_X, ALU.min))

                def hot():
                    routing.done()
                    dve.tensor_tensor(hot_b, over(iota_e8[:, :].unsqueeze(2), [P, E, T]),
                                      over(tiles(first, b).unsqueeze(1), [P, E, T]), ALU.is_equal).then_inc(hot_done, 1)

                def count_seen():
                    dve.wait_ge(hot_done, b + 1)
                    dve.tensor_tensor_scan(seen_b.rearrange("p e t -> p (e t)"), same_e[:, :, :].rearrange("p e t -> p (e t)"),
                                           hot_b.rearrange("p e t -> p (e t)"), 0.0, ALU.mult, ALU.add).then_inc(seen_done, 1)

                def total():
                    dve.wait_ge(seen_done, b + 1)
                    if b == 0:
                        dve.tensor_copy(seen_all[:, 1, :], seen_b[:, :, T - 1]).then_inc(total_done, 1)
                    else:
                        dve.wait_ge(total_done, b)
                        dve.tensor_tensor(seen_all[:, b + 1, :], seen_all[:, b, :], seen_b[:, :, T - 1], ALU.add).then_inc(total_done, 1)

                def its_region():
                    routing.then(dve.tensor_scalar(tiles(region, b), tiles(first, b), float(E), float(REGION), ALU.add, ALU.mult))

                return [largest, where, candidates, lowest, hot, count_seen, total, its_region]

            def places(b):
                def pick():
                    dve.wait_ge(rank_up, b + 1)
                    if b < B - 2:
                        dve.wait_ge(o_up, T * (b + 2) + 3)
                    dve.tensor_tensor(tiles(rank_of, b), rank_psum(b).rearrange("p (e t) -> p t e", e=E),
                                      onehot[:, b].rearrange("p e t -> p t e"), ALU.mult).then_inc(rank_read, 1)

                def add():
                    dve.wait_ge(rank_read, b + 1)
                    routing.then(dve.tensor_reduce(tiles(rank, b), tiles(rank_of, b), AX_X, ALU.add))

                def place_them():
                    routing.done()
                    dve.tensor_tensor(tiles(place, b), tiles(rank, b), tiles(region, b), ALU.add).then_inc(place_done, 1)

                def score():
                    dve.wait_ge(tanh_done, b + 1)
                    dve.tensor_scalar(tiles(zw, b)[:, :, H], tiles(tanh_top, b), 0.5, 0.5, ALU.mult, ALU.add).then_inc(w_done, 1)

                return [pick, add, score, place_them]

            def read_counts():
                counts = M[1][:, T * E:T * E + E]
                dve.wait_ge(rank_up, B)
                dve.tensor_tensor(behind[:, :], counts, region_at[:, :], ALU.add).then_inc(behind_done, 1)
                dve.tensor_scalar(count_up[:, :], counts, (P - 1) / 2, ROUND_P, ALU.add, ALU.add).then_inc(rank_read, 1)

            def slot_tables():
                dve.wait_ge(rank_read, B + 1)
                small.chain(dve.tensor_scalar(slots_128[:, :], count_up[:, :], -ROUND_P, None, ALU.add))
                small.chain(dve.tensor_tensor_scan(end_128[:, :], ones_e[:, :], slots_128[:, :], 0.0, ALU.mult, ALU.add))
                small.chain(dve.tensor_tensor(slot_past[:, :, :], over(end_128[:, :].unsqueeze(1), [P, NS, E]),
                                              over(iota_s[:, :].unsqueeze(2), [P, NS, E]), ALU.is_le))
                small.then(dve.tensor_reduce(slot_exp[:, :], slot_past[:, :, :], AX_X, ALU.add))
                small.chain(dve.tensor_tensor(past_128[:, :, :], slot_past[:, :, :], over(slots_128[:, :].unsqueeze(1), [P, NS, E]),
                                              ALU.mult))
                small.then(dve.tensor_reduce(start_128[:, :], past_128[:, :, :], AX_X, ALU.add))
                small.chain(dve.scalar_tensor_tensor(out=slot_at[:, :], in0=slot_exp[:, :], scalar=float(REGION), in1=iota_s[:, :],
                                                     op0=ALU.mult, op1=ALU.add))
                dve.tensor_tensor(slot_row_i[:, :], slot_at[:, :], start_128[:, :], ALU.subtract).then_inc(srow_done, 1)
                dve.tensor_scalar(slot_exp_i[:, :], slot_exp[:, :], float(E - 1), None, ALU.min).then_inc(sexp_done, 1)

            def weigh_values(lo, hi):
                for b in range(lo, hi):
                    dve.wait_ge(bc_in[b], 16)
                dve.tensor_tensor(wv_ga[:, lo:hi, :], over(wqkv_sb[:, 2:3, :], [P, hi - lo, H]), bc[:, lo:hi, 0, :],
                                  ALU.mult).then_inc(wv_done, 1)

            dve.wait_ge(vec_up, 1)
            dve.tensor_copy(cols[:, :], M[0][:, 0:8]).then_inc(cols_done, 1)
            dve.wait_ge(cols_done, 1)
            dve.tensor_scalar(bq_h[:, :], cols[:, 0:1], 1.0 / H, None, ALU.mult).then_inc(cols_done, 1)
            dve.wait_ge(ld_x[0], 16)
            norm1_stats(0, T, 0)
            for n in range(2, T):
                dve.tensor_scalar(normed[:, n, :], xs[:, n, :], mv1[:, n, 0:1], r1[:, n:n + 1],
                                  ALU.subtract, ALU.mult).then_inc(norm_done, 1)
            dve.wait_ge(modc_up, 1)
            dve.tensor_copy(shift_a[:, :], M[1][:, 0:B]).then_inc(modc_done, 1)
            dve.tensor_scalar(scale_a[:, :], M[1][:, B:2 * B], 1.0, None, ALU.add).then_inc(modc_done, 1)
            dve.wait_ge(modr_up, 1)
            dve.tensor_copy(mod_raw[:, :, :], PT[0][0:B, :].rearrange("p (j h) -> p j h", j=4)).then_inc(modr_raw, 1)
            dve.wait_ge(modr_raw, 1)
            gates = mod_raw[:, 0:4:3, :]
            small.then(dve.tensor_scalar(gate_sign[:, :, :], gates, 0.0, -0.5, ALU.is_ge, ALU.add))
            small.chain(dve.scalar_tensor_tensor(out=gate_abs[:, :, :], in0=gates, scalar=-1.0, in1=gates, op0=ALU.mult, op1=ALU.max))
            small.chain(dve.scalar_tensor_tensor(out=gate_half[:, :, :], in0=gate_abs[:, :, :], scalar=0.25, in1=gate_sign[:, :, :],
                                                 op0=ALU.max, op1=ALU.mult))
            dve.tensor_scalar(mod_rows[:, 0:2, :], gate_half[:, :, :], 2.0, None, ALU.mult).then_inc(modr_done, 1)
            dve.tensor_copy(mod_rows[:, 2, :], mod_raw[:, 1, :]).then_inc(modr_done, 1)
            dve.tensor_scalar(mod_rows[:, 3, :], mod_raw[:, 2, :], 1.0, None, ALU.add).then_inc(modr_done, 1)
            dve.wait_ge(ld_bv, 16)
            dve.wait_ge(modr_done, 1)
            dve.tensor_tensor(mod_rows[:, 4, :], mod_rows[:, 0, :], bv_rows[:, :], ALU.mult).then_inc(modr_done, 1)
            dve.wait_ge(ld_x[1], 16)
            norm1_stats(T, 2 * T, 1)
            dve.wait_ge(c_done, CONSTS)
            score_max(0)
            weigh_values(0, 1)
            score_max(1)
            invert_sum(0)
            for b in range(B):
                n = T * b
                nxt = b + 1 < B
                route = routes(b - 2) if b >= 2 else []
                if b >= 1:
                    norm2(b - 1, before=[lambda: score_max(n + 2)],
                          between=[lambda: invert_sum(n + 1)] + route[0:4] + [lambda: score_max(n + 3)])
                    attention_out(n)
                else:
                    score_max(n + 2)
                    weigh_values(1, B)
                    score_max(n + 3)
                    invert_sum(n + 1)
                    attention_out(n)
                for step in route[4:6]:
                    step()
                invert_sum(n + 2)
                attention_out(n + 1)
                if b >= 1:
                    norm3(b - 1, between=route[6:] + (places(b - 2) if b >= 2 else []) + [lambda: attention_out(n + 2), lambda: invert_sum(n + 3)])
                else:
                    attention_out(n + 2)
                    invert_sum(n + 3)
                    dve.wait_ge(ld_x[2], 16)
                    dve.wait_ge(ld_x[3], 16)
                    norm1_stats(2 * T, NT, 2, between=[lambda: attention_out(n + 3), lambda: score_max(n + T), lambda: score_max(n + T + 1)])
                if b >= 1:
                    attention_out(n + 3)
                if nxt and b >= 1:
                    score_max(n + T)
                    score_max(n + T + 1)
                if nxt:
                    invert_sum(n + T)
            norm2(B - 1)
            norm3(B - 1, between=routes(B - 2))
            for step in places(B - 2):
                step()
            shared_out(0)
            shared_hidden(4)
            dve.wait_ge(xf_hi_done, B)
            dve.tensor_tensor(xf_lo[:, B - 1, :], xfT[:, :], xf_hi[:, B - 1, :].bitcast(F32), ALU.subtract).then_inc(xf_split, 1)
            for step in routes(B - 1):
                step()
            for step in places(B - 1):
                step()
            read_counts()
            shared_hidden(5)
            slot_tables()
            shared_out(1)
            shared_hidden(6)
            shared_hidden(7)
            shared_out(2)
            shared_out(3)
            def slot_split(s):
                if s >= 3:
                    dve.wait_ge(gu_up, s - 2)
                dve.wait_ge(xs_done, s + 1)
                dve.tensor_copy(xs_hi[:, s % 3, :], xsT[:, s % 3, :]).then_inc(xhi_done, 1)
                dve.wait_ge(xhi_done, s + 1)
                dve.tensor_tensor(xs_lo[:, s % 3, :], xsT[:, s % 3, :], xs_hi[:, s % 3, :].bitcast(F32),
                                  ALU.subtract).then_inc(xlo_done, 1)

            slot_split(0)
            for s in range(NS + 3):
                if s + 1 < NS:
                    slot_split(s + 1)
                if s < NS:
                    dve.wait_ge(ss_done, s + 1)
                    if s >= 2:
                        dve.wait_ge(ht_up, s - 1)
                    dve.scalar_tensor_tensor(out=sl_hid[:, s % 2, :], in0=S[s % 2][:, I:2 * I], scalar=zw[:, s, H:H + 1],
                                             in1=sl_silu[:, s % 2, :], op0=ALU.mult, op1=ALU.mult).then_inc(sh_done, 1)
                if s >= 3:
                    k = s - 3
                    dve.wait_ge(y_up, k + 1)
                    dve.tensor_tensor(y_sl[:, k, :], O[k % 2][:, 0:H], zw[:, k, H + 1:2 * H + 1], ALU.mult).then_inc(y_done, 1)

        @block.tensor
        def _(pe):
            def transposes(dst, src_of, count):
                for t in range(count):
                    last = pe.transpose(dst[:, t * P:(t + 1) * P], src_of(t), ident[:, :])
                return last

            def split_product(dst, l_hi, l_lo, r_hi, r_lo):
                pe.matmul(dst, l_hi, r_hi, start=True, stop=False)
                pe.matmul(dst, l_hi, r_lo, start=False, stop=False)
                return pe.matmul(dst, l_lo, r_hi, start=False, stop=True)

            def rows_T(b):
                pe.wait_ge(norm_done, T * (b + 1))
                if b >= 3:
                    pe.wait_ge(xfT_done, b - 2)
                elif b >= 1:
                    pe.wait_ge(kT_done, b)
                else:
                    pe.wait_ge(cols_done, 1)
                transposes(M[0], lambda t: normed[:, t, :], T).then_inc(nT_up, 1)

            def q_product(b):
                pe.wait_ge(hT_done, b + 1)
                if b >= 3:
                    pe.wait_ge(lg_done, b - 2)
                elif b >= 1:
                    pe.wait_ge(v_done, b)
                else:
                    pe.wait_ge(modc_done, 2)
                pe.matmul(M[1][:, :], wqkv_sb[:, 0, :], hT[:, :], start=True, stop=True).then_inc(q_up, 1)

            def k_product(b):
                pe.matmul(M[0][:, :], wqkv_sb[:, 1, :], hT[:, :], start=True, stop=True).then_inc(k_up, 1)

            def v_product(b):
                pe.wait_ge(qT_done, b + 1)
                pe.wait_ge(wv_done, 1 if b == 0 else 2)
                for t in range(T):
                    last = pe.matmul(M[1][:, t * H:(t + 1) * H], hT[:, t * P:(t + 1) * P], wv_ga[:, b, :], start=True, stop=True)
                last.then_inc(v_up, 1)

            def scores(n):
                b, t = n // T, n % T
                if t == 0:
                    pe.wait_ge(kT_done, b + 1)
                if n >= 2:
                    pe.wait_ge(p_done, n - 1)
                pe.matmul(S[n % 2][:, :], qT[:, t * P:(t + 1) * P], kT[:, :], start=True, stop=False)
                pe.matmul(S[n % 2][:, t * P:(t + 1) * P], ident_b[:, :], mask_diag[:, :], start=False, stop=True).then_inc(s_up, 1)

            def probs_up(n):
                pe.wait_ge(p_done, n + 1)
                if n >= 2:
                    pe.wait_ge(pT_done, n - 1)
                transposes(PT[n % 2], lambda k: probs[:, n % 2, k * P:(k + 1) * P], T).then_inc(pT_up, 1)

            def attend(n):
                pe.wait_ge(pT_done, n + 1)
                if n % T == 0:
                    pe.wait_ge(v_done, n // T + 1)
                if n >= 2:
                    pe.wait_ge(x1_done, n - 1)
                if n % T == 0 and n // T == B - 1:
                    pe.wait_ge(rank_read, B - 3)
                for k in range(T):
                    last = pe.matmul(O[n % 2][:, 0:H], probsT[:, n % 2, k * P:(k + 1) * P], v_sb[:, n // T % 2, k, :], start=(k == 0), stop=(k == T - 1))
                last.then_inc(o_up, 1)

            def z_T(b):
                pe.wait_ge(z_done, T * (b + 1))
                if b + 2 < B:
                    pe.wait_ge(kT_done, b + 3)
                else:
                    pe.wait_ge(xfT_done, b)
                    pe.wait_ge(shsilu_done, 1)
                transposes(M[0], lambda t: zw[:, T * b + t, 0:H], T).then_inc(zT_up, 1)

            def logits(b):
                pe.wait_ge(xfT_done, b + 1)
                if b + 2 < B:
                    pe.wait_ge(v_done, b + 3)
                elif b == B - 2:
                    pe.wait_ge(shup_done, 1)
                else:
                    pe.wait_ge(rank_read, b)
                for t in range(T):
                    last = pe.matmul(M[1][:, t * E:(t + 1) * E], xfT[:, t * P:(t + 1) * P], router_sb[:, :], start=True, stop=True)
                last.then_inc(lg_up, 1)

            def rank_product(b):
                if b < B - 2:
                    pe.wait_ge(x1_done, T * (b + 2) + 1)
                else:
                    pe.wait_ge(lg_done, b + 1)
                r = rank_psum(b)
                pe.wait_ge(hot_done, b + 1)
                pe.matmul(r, not_before[:, :], onehot[:, b].rearrange("p e t -> p (e t)"), start=True, stop=False)
                pe.wait_ge(seen_done, b + 1)
                if b >= 1:
                    pe.wait_ge(total_done, b)
                    pe.matmul(r, ones_b[:, :], over(seen_all[:, b, :].unsqueeze(2), [P, E, T]), start=False, stop=False)
                last = pe.matmul(r, ones_b[:, :], seen[:, b].rearrange("p e t -> p (e t)"), start=False, stop=True)
                if b == B - 1:
                    pe.wait_ge(total_done, B)
                    last = pe.matmul(M[1][:, T * E:T * E + E], ones_b[:, :], seen_all[:, B, :], start=True, stop=True)
                last.then_inc(rank_up, 1)

            def shared_in(k):
                b, c = k // IC, k % IC
                gate, up = SH_BANKS[k]
                if k == 0:
                    pe.wait_ge(sh_lo_done, 1)
                    pe.wait_ge(lg_done, B - 2)
                    pe.wait_ge(xfT_done, B - 2)
                elif k == 1:
                    pe.wait_ge(p_done, NT)
                elif k == 2:
                    pe.wait_ge(pT_done, NT)
                else:
                    pe.wait_ge(shhid_done[k - 2], 1)
                if c == 0:
                    pe.wait_ge(xf_split, b + 1)
                cg, cu = slice(c * P, (c + 1) * P), slice(I + c * P, I + (c + 1) * P)
                split_product(gate[:, :], sh_gu_hi[:, cg], sh_gu_lo[:, cg], xf_hi[:, b, :], xf_lo[:, b, :]).then_inc(shg_up, 1)
                split_product(up[:, :], sh_gu_hi[:, cu], sh_gu_lo[:, cu], xf_hi[:, b, :], xf_lo[:, b, :]).then_inc(shu_up, 1)

            def shared_out(b):
                for c in range(IC):
                    pe.wait_ge(shhid_done[IC * b + c], 1)
                pe.wait_ge(shd_done, b + 1)
                if b >= 2:
                    pe.wait_ge(base_done, b - 1)
                else:
                    pe.wait_ge(x1_done, NT)
                    pe.wait_ge(rank_read, B - 2)
                for t in range(T):
                    for c in range(IC):
                        last = pe.matmul(O[b % 2][:, t * H:(t + 1) * H], sh_hid[:, (IC * b + c) % 4, t * P:(t + 1) * P], sh_down_gb[:, b, c, :],
                                         start=(c == 0), stop=(c == IC - 1))
                last.then_inc(shd_up, 1)

            def keep_warm(count, bank=O[0]):
                for _ in range(count):
                    pe.matmul(bank[:, :], warm[:, 0:P], warm[:, :], start=True, stop=True)

            pe.wait_ge(c_set, 1)
            keep_warm(WARM[0])
            pe.wait_ge(ld_vec, 16)
            pe.wait_ge(c_done, 1)
            pe.transpose(M[0][:, 0:8], vec_rows[:, :], ident[0:8, 0:8]).then_inc(vec_up, 1)
            keep_warm(WARM[1])
            pe.wait_ge(silu_done, 1)
            pe.wait_ge(ld_wmod, 16)
            for j in range(2):
                last = pe.matmul(M[1][:, j * B:(j + 1) * B], wmod_sb[:, j * H:(j + 1) * H], silu_c[:, :], start=True, stop=True)
            last.then_inc(modc_up, 1)
            pe.matmul(PT[0][0:B, :], silu_c[:, :], wmod_sb[:, 2 * H:6 * H], start=True, stop=True).then_inc(modr_up, 1)
            keep_warm(WARM[2])
            rows_T(0)
            keep_warm(WARM[3])
            pe.wait_ge(ld_wqkv, 16)
            q_product(0)
            k_product(0)
            keep_warm(WARM[4])
            pe.wait_ge(c_done, CONSTS)
            scores(0)
            scores(1)
            v_product(0)
            for b in range(B):
                n = T * b
                nxt = b + 1 < B
                probs_up(n)
                scores(n + 2)
                if b >= 2:
                    logits(b - 2)
                attend(n)
                probs_up(n + 1)
                if nxt:
                    rows_T(b + 1)
                scores(n + 3)
                attend(n + 1)
                probs_up(n + 2)
                if nxt:
                    q_product(b + 1)
                else:
                    shared_in(0)
                if b >= 2:
                    rank_product(b - 2)
                attend(n + 2)
                if nxt:
                    k_product(b + 1)
                probs_up(n + 3)
                if nxt:
                    v_product(b + 1)
                else:
                    shared_in(1)
                attend(n + 3)
                if nxt:
                    scores(n + T)
                    scores(n + T + 1)
                if b == 1:
                    pe.wait_ge(ld_router, 16)
                if b >= 1:
                    z_T(b - 1)
            shared_in(2)
            logits(B - 2)
            shared_in(3)
            shared_out(0)
            shared_in(4)
            keep_warm(WARM[7], O[1])
            rank_product(B - 2)
            keep_warm(WARM[8], O[1])
            z_T(B - 1)
            shared_in(5)
            logits(B - 1)
            shared_out(1)
            rank_product(B - 1)
            shared_in(6)
            shared_in(7)
            shared_out(2)
            shared_out(3)

            pe.wait_ge(sexp_done, 1)
            _, expert = nc.values_load_multi_w_load_instructions(
                slot_exp_i[0:1, :], engines=(mybir.EngineType.PE,), min_val=0, max_val=E - 1,
                skip_runtime_bounds_check_because="min with E - 1 of a sum of comparisons")

            def slot_T(s):
                pe.wait_ge(slot_in_sem[s], 16)
                if s >= 2:
                    pe.wait_ge(xs_done, s - 1)
                else:
                    pe.wait_ge(xfT_done, B)
                pe.transpose(M[s % 2][:, 0:P], zw[:, s, 0:H], ident[:, :]).then_inc(xs_up, 1)

            def slot_in(s):
                pe.wait_ge(xlo_done, s + 1)
                if s >= 2:
                    pe.wait_ge(sh_done, s - 1)
                else:
                    pe.wait_ge(shhid_done[2 * B - 1], 1)
                cols_e = bass.ds(expert[s] * (2 * I), 2 * I)
                split_product(S[s % 2][:, :], xs_hi[:, s % 3, :], xs_lo[:, s % 3, :], w_gu_hi[:, cols_e], w_gu_lo[:, cols_e]
                              ).then_inc(gu_up, 1)

            def slot_hid_T(s):
                pe.wait_ge(sh_done, s + 1)
                if s >= 2:
                    pe.wait_ge(ht_done, s - 1)
                transposes(PT[s % 2], lambda c: sl_hid[:, s % 2, c * P:(c + 1) * P], IC).then_inc(ht_up, 1)

            def slot_out(s):
                pe.wait_ge(ht_done, s + 1)
                if s >= 2:
                    pe.wait_ge(y_done, s - 1)
                else:
                    pe.wait_ge(base_done, B)
                for c in range(IC):
                    last = pe.matmul(O[s % 2][:, 0:H], sl_hidT[:, s % 3, c, :],
                                     w_down_sb[:, bass.ds(expert[s] * (IC * H) + c * H, H)], start=(c == 0), stop=(c == IC - 1))
                last.then_inc(y_up, 1)

            pe.wait_ge(base_done, B - 1)
            keep_warm(WARM[5])
            slot_T(0)
            slot_T(1)
            pe.wait_ge(w_lo_done, B)
            pe.wait_ge(ld_down, 16)
            keep_warm(WARM[6])
            for s in range(NS + 3):
                if s < NS:
                    slot_in(s)
                if s + 2 < NS:
                    slot_T(s + 2)
                if s >= 3:
                    slot_out(s - 3)
                if 1 <= s <= NS:
                    slot_hid_T(s - 1)


def kernel(**inputs):
    import numpy as np
    import concourse.bacc as bacc
    from concourse.bass_utils import run_bass_kernel_spmd

    a = {k.removeprefix("L0_"): np.asarray(v) for k, v in inputs.items()}
    side_by_side = lambda g, u, axis: np.concatenate([g, u], axis=axis)
    arrays = {
        "x": a["attn_x"].reshape(B * L, H),
        "vecs": np.concatenate([np.stack([a["attn_bq"], a["attn_bk"], a["ffn_ln_w"], a["ffn_ln_b"]]), a["c"]]),
        "bv": a["attn_bv"],
        "wmod": a["wmod"],
        "wqkv": np.stack([a["attn_Wq"].T, a["attn_Wk"].T, a["attn_Wv"].T], axis=1),
        "router_w": a["ffn_router_w"],
        "w_gu": side_by_side(a["ffn_gate_w"], a["ffn_up_w"], 2).transpose(1, 0, 2).reshape(H, E * 2 * I),
        "w_down": a["ffn_down_w"].reshape(E, IC, P, H).transpose(2, 0, 1, 3).reshape(P, E * IC * H),
        "sh_gu": side_by_side(a["ffn_sh_gate"], a["ffn_sh_up"], 1),
        "sh_down": a["ffn_sh_down"].reshape(IC, P, H).transpose(1, 0, 2),
    }
    arrays = {f"in_{k}": np.ascontiguousarray(v) for k, v in arrays.items()}
    nc = bacc.Bacc("TRN2", target_bir_lowering=False, num_devices=1)
    args = [nc.dram_tensor(k, v.shape, mybir.dt.from_np(v.dtype), kind="ExternalInput").ap() for k, v in arrays.items()]
    out = nc.dram_tensor("out_0", (B * L + SPARE * P, H), F32, kind="ExternalOutput").ap()
    adaln_block(nc, *args, out)
    r = run_bass_kernel_spmd(nc, [arrays], core_ids=[0])
    return r.results[0]["out_0"][:B * L].reshape(B, L, H)
```
